# Optimizing a Trainium2 kernel written in Bass

```python
import numpy as np
import jax
import jax.numpy as jnp

def _softmax(x, axis=-1):
    return jax.nn.softmax(x, axis=axis)

def _gelu(x):
    return jax.nn.gelu(x, approximate=True)

def _silu(x):
    return jax.nn.silu(x)

def _sigmoid(x):
    return jax.nn.sigmoid(x)

def _layernorm(x, axis=-1, eps=1e-05):
    m = jnp.mean(x, axis=axis, keepdims=True)
    v = jnp.var(x, axis=axis, keepdims=True)
    return (x - m) / jnp.sqrt(v + eps)

def _scatter_add(tgt, idx, src, axis=0):
    return tgt.at[idx].add(src)

def _segment_sum(src, seg, n):
    return jax.ops.segment_sum(src, seg, n)
kernel_name = 'mk_adaln_attn_ffn_d1_seqx_r4_ed4c62'

def setup_inputs(seed: int=0):
    np.random.seed(seed)
    _w = jnp.asarray

    def _rec_inputs():
        import jax
        import jax.numpy as jnp
        _rk = jax.random.key(seed)
        x = -7.109e-05 + 0.9999 * jax.random.normal(jax.random.fold_in(_rk, 1), (128, 64, 1024), jnp.float32)
        _lenS = 64 - jax.random.randint(jax.random.fold_in(_rk, 7), (128,), 0, max(1, 64 // 4) + 1, jnp.int32)
        _lenS2 = 64 - jax.random.randint(jax.random.fold_in(_rk, 8), (128,), 0, max(1, 64 // 4) + 1, jnp.int32)
        itok_B_0_15 = jax.random.randint(jax.random.fold_in(_rk, 11), (128,), 0, 16, jnp.int32)
        return (x, itok_B_0_15)
    x, itok_B_0_15 = _rec_inputs()

    def _L0_cond_setup():
        import jax, jax.numpy as jnp
        import numpy as np
        NUM_CONDITIONS = 16
        IN_CH = 64
        OUT_CH = 64
        B = 64
        T = 1024
        key = jax.random.key(seed)
        k_x, k_w, k_c = jax.random.split(key, 3)
        x = jax.random.normal(k_x, (B, IN_CH, T), dtype=jnp.float32)
        bound = float(np.sqrt(6.0 / IN_CH))
        weights = jax.random.uniform(k_w, (NUM_CONDITIONS, IN_CH, OUT_CH), dtype=jnp.float32, minval=-bound, maxval=bound)
        condition = jax.random.randint(k_c, (B,), 0, NUM_CONDITIONS, dtype=jnp.int64)
        return {'x': x, 'weights': weights, 'condition': condition}
    _L0_cond_all = _L0_cond_setup()
    _L0_cond_in = {k: v for k, v in _L0_cond_all.items() if k in ('weights',)}
    del _L0_cond_all

    def _L0_attn_setup():
        import jax, jax.numpy as jnp
        import numpy as np
        H = 1024
        D = H // 4
        key = jax.random.key(seed)
        k1, k2, k3, k4, k5 = jax.random.split(key, 5)
        x = jax.random.normal(k1, (4, 1024, H), dtype=jnp.float32)
        s_in = 1.0 / np.sqrt(H)
        Wqkv = jax.random.normal(k2, (H, 3 * D), dtype=jnp.float32) * s_in
        bqkv = jax.random.normal(k3, (3 * D,), dtype=jnp.float32) * 0.01
        Wo = jax.random.normal(k4, (D, H), dtype=jnp.float32) * (1.0 / np.sqrt(D))
        bo = jax.random.normal(k5, (H,), dtype=jnp.float32) * 0.01
        return {'x': x, 'Wqkv': Wqkv, 'bqkv': bqkv, 'Wo': Wo, 'bo': bo}
    _L0_attn_all = _L0_attn_setup()
    _L0_attn_in = {k: v for k, v in _L0_attn_all.items() if k in ('Wqkv', 'bqkv', 'Wo', 'bo')}
    del _L0_attn_all

    def _L0_cond2_setup():
        import jax, jax.numpy as jnp
        import numpy as np
        MAX_LORAS = 16
        IN, OUT = (1024, 1024)
        B, S = (8, 512)
        key = jax.random.key(seed)
        k1, k2, k3 = jax.random.split(key, 3)
        x = jax.random.normal(k1, (B, S, IN), dtype=jnp.float32)
        adapter_ids = jax.random.randint(k2, (B,), 0, MAX_LORAS)
        weight = jax.random.normal(k3, (MAX_LORAS, OUT, IN), dtype=jnp.float32) * 0.02
        return {'x': x, 'adapter_ids': adapter_ids, 'weight': weight}
    _L0_cond2_all = _L0_cond2_setup()
    _L0_cond2_in = {k: v for k, v in _L0_cond2_all.items() if k in ('weight',)}
    del _L0_cond2_all

    def _L0_ffn_setup():
        import jax, jax.numpy as jnp
        import numpy as np
        RANKS = (8, 16, 32, 64)
        TOPK = 1
        SCALING = 1.0 / 4
        key = jax.random.key(seed)
        ks = jax.random.split(key, 7)
        D_IN, D_OUT, MAX_R, N_RANKS = (1024, 1024, 64, len(RANKS))
        B_, S_ = (4, 512)
        return {'hidden_states': jax.random.normal(ks[0], (B_, S_, D_IN), jnp.float32), 'W': jax.random.normal(ks[1], (D_OUT, D_IN), jnp.float32) * 0.02, 'b': jax.random.normal(ks[2], (D_OUT,), jnp.float32) * 0.02, 'A': jax.random.normal(ks[3], (MAX_R, D_IN), jnp.float32) * 0.02, 'B': jnp.zeros((D_OUT, MAX_R), jnp.float32) + jax.random.normal(ks[4], (D_OUT, MAX_R), jnp.float32) * 0.02, 'gate_w': jax.random.normal(ks[5], (N_RANKS, D_IN), jnp.float32) * 0.02, 'gate_b': jax.random.normal(ks[6], (N_RANKS,), jnp.float32) * 0.02}
    _L0_ffn_all = _L0_ffn_setup()
    _L0_ffn_in = {k: v for k, v in _L0_ffn_all.items() if k in ('W', 'b', 'A', 'B', 'gate_w', 'gate_b')}
    del _L0_ffn_all
    return {'x': x, 'itok_B_0_15': itok_B_0_15, 'L0_cond_weights': _L0_cond_in['weights'], 'L0_attn_Wqkv': _L0_attn_in['Wqkv'], 'L0_attn_bqkv': _L0_attn_in['bqkv'], 'L0_attn_Wo': _L0_attn_in['Wo'], 'L0_attn_bo': _L0_attn_in['bo'], 'L0_cond2_weight': _L0_cond2_in['weight'], 'L0_ffn_W': _L0_ffn_in['W'], 'L0_ffn_b': _L0_ffn_in['b'], 'L0_ffn_A': _L0_ffn_in['A'], 'L0_ffn_B': _L0_ffn_in['B'], 'L0_ffn_gate_w': _L0_ffn_in['gate_w'], 'L0_ffn_gate_b': _L0_ffn_in['gate_b']}

def reference(x, itok_B_0_15, L0_cond_weights, L0_attn_Wqkv, L0_attn_bqkv, L0_attn_Wo, L0_attn_bo, L0_cond2_weight, L0_ffn_W, L0_ffn_b, L0_ffn_A, L0_ffn_B, L0_ffn_gate_w, L0_ffn_gate_b):
    import jax
    import jax.numpy as jnp

    def _L0_cond_ref(x, weights, condition):
        import jax, jax.numpy as jnp
        import numpy as np
        NUM_CONDITIONS = 16
        IN_CH = 64
        OUT_CH = 64
        B = 64
        T = 1024
        W = weights[condition]
        return jnp.einsum('bct,bcd->bdt', x, W)

    def _L0_attn_ref(x, Wqkv, bqkv, Wo, bo):
        import jax, jax.numpy as jnp
        import numpy as np
        H = 1024
        D = H // 4
        B, S, C = x.shape
        d = C // 4
        qkv = jnp.einsum('bsc,cf->bsf', x, Wqkv) + bqkv
        qkv = qkv.reshape(B, S, 3, d)
        q, k, v = (qkv[:, :, 0], qkv[:, :, 1], qkv[:, :, 2])
        scale = 1.0 / jnp.sqrt(jnp.float32(d)).astype(x.dtype)
        attn = jnp.einsum('bqd,bkd->bqk', q, k) * scale
        attn = jax.nn.softmax(attn, axis=-1)
        out = jnp.einsum('bqk,bkd->bqd', attn, v)
        return jnp.einsum('bqd,dc->bqc', out, Wo) + bo

    def _L0_cond2_ref(x, adapter_ids, weight):
        import jax, jax.numpy as jnp
        import numpy as np
        MAX_LORAS = 16
        IN, OUT = (1024, 1024)
        B, S = (8, 512)
        w = weight[adapter_ids]
        return jnp.einsum('bsi,boi->bso', x, w)

    def _L0_ffn_ref(hidden_states, W, b, A, B, gate_w, gate_b):
        import jax, jax.numpy as jnp
        import numpy as np
        RANKS = (8, 16, 32, 64)
        TOPK = 1
        SCALING = 1.0 / 4
        bsz, seq, d_in = hidden_states.shape
        out = jnp.einsum('bsd,od->bso', hidden_states, W) + b
        x = hidden_states.reshape(-1, d_in)
        scores = x @ gate_w.T + gate_b
        probs = jax.nn.softmax(scores, axis=-1)
        routing_weights, selected = jax.lax.top_k(probs, TOPK)
        routing_weights = routing_weights / jnp.sum(routing_weights, axis=-1, keepdims=True)
        lora_outputs = jnp.stack([x @ A[:r, :].T @ B[:, :r].T for r in RANKS], axis=1)
        sel = jnp.take_along_axis(lora_outputs, selected[:, :, None], axis=1)
        final = jnp.sum(sel * routing_weights[:, :, None], axis=1)
        return out + final.reshape(bsz, seq, -1)
    x = x + _L0_attn_ref(_L0_cond_ref(x, L0_cond_weights, itok_B_0_15), L0_attn_Wqkv, L0_attn_bqkv, L0_attn_Wo, L0_attn_bo)
    x = x + _L0_ffn_ref(_L0_cond2_ref(x, itok_B_0_15, L0_cond2_weight), L0_ffn_W, L0_ffn_b, L0_ffn_A, L0_ffn_B, L0_ffn_gate_w, L0_ffn_gate_b)
    return x

_drawn_inputs = setup_inputs


def setup_inputs(seed=0):
    import zlib

    import numpy as np

    out = dict(_drawn_inputs(seed))
    spreads = {}
    factors = {'L0_attn_bqkv': 5.138, 'L0_attn_bo': 6.374, 'L0_ffn_b': 3.541, 'L0_ffn_gate_b': 29.758}
    for name, (base, spread) in spreads.items():
        noise = np.random.default_rng([zlib.crc32(name.encode()), seed]).standard_normal(out[name].shape)
        drawn = base * np.exp(spread * noise) if base else spread * noise
        out[name] = jnp.asarray(drawn.astype(out[name].dtype))
    for name, factor in factors.items():
        out[name] = (out[name] * factor).astype(out[name].dtype)
    return out
```

```python
from contextlib import ExitStack

import concourse.bass as bass
from concourse import mybir

F32, F16, I32 = mybir.dt.float32, mybir.dt.float16, mybir.dt.int32
ALU = mybir.AluOpType
ACT = mybir.ActivationFunctionType
AX = mybir.AxisListType

P = 128
S = 64
T = 1024
K = T // P
DH = 256
NC = 16
R = 64
RANKS = (8, 16, 32, 64)
G4 = len(RANKS)
RG = R + G4
BT = K * S
PT2 = 2 * BT
GR = 2 * PT2
RING = 4
STAGE = 4

SX = 16.0
SZ = 4.0
SC = 16.0
SW = 256.0
SP = 256.0
SU = 32.0
SO = SZ * SU
SQ = SZ * SC

EXP_SCALE = 1.0 / (SQ * SQ * DH ** 0.5)
MASKED = -1.0e30

B_QK, B_V, B_O, B_F, NBIAS = 0, 4, 6, 14, 22


def wait(eng, sem, i, a, b):
    if isinstance(i, int):
        if a * i + b > 0:
            eng.wait_ge(sem, a * i + b)
    else:
        assert a + b > 0, "the first looped step would wait for nothing: peel it"
        eng.wait_ge(sem, a * i + b)


def build(nc, NB, x_in, ids_in, wc_in, wqkv_in, wo_in, w2_in, w_in, ag_in, bl_in, bias_in, gb_in, out, x1):
    NP = NB // 2
    GA = NP // 2
    IA = GA // 2
    SLOT = NB + NC
    NSL = SLOT // 2
    GB = NSL // 2
    IB = GB // 2
    assert GA % RING == 0 and GB % 2 == 0 and NB <= P
    FA = 8 * GA

    ctx = ExitStack()
    with ctx:
        def sb(name, shape, dt):
            return ctx.enter_context(nc.sbuf_tensor(name, shape, dt))

        def sem(name):
            return ctx.enter_context(nc.semaphore(name))

        xr = sb("xr", [P, RING * GR], F32)
        stage = sb("stage", [P, STAGE, T], F32)
        w2 = sb("w2", [P, 2, 2 * K * T], F16)
        wf = sb("wf", [P, 2 * K * T], F16)
        wf_h = wf[:, 0:K * T].rearrange("p (k n) -> p k n", k=K)
        wf_l = wf[:, K * T:].rearrange("p (k n) -> p k n", k=K)
        NQ = 3 * DH
        wa = w2[:, 1, :]
        wq_h = wa[:, 0:K * NQ].rearrange("p (k n) -> p k n", k=K)
        wq_l = wa[:, K * NQ:2 * K * NQ].rearrange("p (k n) -> p k n", k=K)
        o0 = 2 * K * NQ
        wo_h = wa[:, o0:o0 + 2 * T].rearrange("p (k n) -> p k n", k=2)
        wo_l = wa[:, o0 + 2 * T:o0 + 4 * T].rearrange("p (k n) -> p k n", k=2)
        ag = sb("ag", [P, K, 2 * RG], F16)
        bl_h = sb("bl_h", [P, T], F16)
        bl_l = sb("bl_l", [P, T], F16)
        xs = sb("xs", [P, 2, K, 2 * P], F16)
        zh_flat = sb("zh", [P, 2 * NQ], F16)
        zl_flat = sb("zl", [P, 2 * NQ], F16)
        zh = zh_flat[:, :].rearrange("p (r n) -> p r n", r=2)
        zl = zl_flat[:, :].rearrange("p (r n) -> p r n", r=2)
        qkh = sb("qkh", [P, 4, P], F16)
        qkl = sb("qkl", [P, 4, P], F16)
        wcf = sb("wcf", [P, 4, 2 * P], F32)
        wch = sb("wch", [P, 2, 2 * P], F16)
        wcl = sb("wcl", [P, 2, 2 * P], F16)
        sm = sb("sm", [P, P], F32)
        ex = sb("ex", [P, P], F32)
        pn = sb("pn", [P, P], F32)
        soft = sb("soft", [P, 4], F32)
        pth = sb("pth", [P, P], F16)
        ptl = sb("ptl", [P, P], F16)
        uh = sb("uh", [P, P], F16)
        ul = sb("ul", [P, P], F16)
        oh = sb("oh", [P, 2, 2, 2 * P], F16)
        ol = sb("ol", [P, 2, 2, 2 * P], F16)
        ft = sb("ft", [P, 2, 2 * P], F32)
        tt = zh_flat[:, 0:8 * P].bitcast(F32).rearrange("p (r m n) -> p r m n", r=2, m=2)
        yf = zl_flat[:, 0:8 * P].bitcast(F32).rearrange("p (r m n) -> p r m n", r=2, m=2)
        yh = sb("yh", [P, 2, K, 2 * P], F16)
        yl_flat = sb("yl", [P, 4 * K * P], F16)
        yl = yl_flat[:, :].rearrange("p (r k n) -> p r k n", r=2, k=K)
        gt = sb("gt", [P, RG], F32)
        gs = sb("gs", [P, 2, RG], F32)
        gb = sb("gb", [P, 2, G4], F32)
        sc = sb("sc", [P, 2, G4], F32)
        pm = sb("pm", [P, 2, 2], F32)
        m012 = sb("m012", [P, 2, 1], F32)
        m123 = sb("m123", [P, 2, 1], F32)
        mx = sb("mx", [P, 2, 1], F32)
        dd = sb("dd", [P, 2, G4], F32)
        ee = sb("ee", [P, 2, G4], F32)
        den = sb("den", [P, 2], F32)
        ptop = sb("ptop", [P, 2], F32)
        itop = sb("itop", [P, 2], F32)
        cw = sb("cw", [P, 2, G4], F32)
        mf = sb("mf", [P, 2, R], F32)
        mhl = sb("mhl", [P, 2, 2 * R], F16)
        mT = sb("mT", [P, 2 * P], F16)
        bias = sb("bias", [P, NBIAS], F32)
        biasq = sb("biasq", [P, 6], F32)
        ident = sb("ident", [P, P], F32)
        ident16 = sb("ident16", [P, P], F16)
        mask = sb("mask", [P, P], F32)
        scratch = yl_flat[:, :].bitcast(F32)
        taken = [0]

        def carve(rows_, n):
            taken[0] += n
            assert taken[0] <= 2 * K * P
            return scratch[0:rows_, taken[0] - n:taken[0]]

        idc_i = sb("idc_i", [P, 1], I32)
        idr_i = sb("idr_i", [P, NB], I32)
        cols = sb("cols", [P, 3], F32)
        idr = carve(P, NB)
        ones = sb("ones", [P, P], F32)
        lower = carve(P, NB)
        tri = sb("tri", [NC, 2 * NC], F32)
        iota_e = sb("iota_e", [P, NC], F32)
        iota_s = carve(P, SLOT)
        spare = carve(1, SLOT)
        rank = sb("rank", [P, 3], F32)
        hot = carve(P, SLOT)
        cnt_i = sb("cnt_i", [NC, 2], I32)
        cnt = sb("cnt", [NC, 3], F32)
        pcb = carve(NC, P)
        rows = carve(1, 5 * SLOT)
        order = sb("order", [1, 3 * SLOT + NC], I32)
        SRC, DST, CND, CUM = 0, SLOT, 2 * SLOT, 3 * SLOT

        bank = [ctx.enter_context(nc.psum_tensor(f"bank{n}", [P, 512], F32)) for n in range(8)]
        zps = [[bank[0], bank[1]], [bank[2], bank[3]]]
        qkps, chps, wops = bank[4], bank[5], [bank[6], bank[7]]
        c2ps, fps, gps, trps = bank[0:4], [bank[4], bank[5]], bank[6], bank[7]
        mtps = trps[:, 0:P].bitcast(F16)

        s_ids, s_small = sem("ids_loaded"), sem("small_loaded")
        s_stage = [sem(f"stage{n}_loaded") for n in range(STAGE)]
        s_pst = [sem(f"pool_stage{n}_loaded") for n in range(STAGE)]
        s_wh, s_wl = sem("weight_hi_made"), sem("weight_lo_made")
        s_pc, s_pw = sem("pool_hi_scaled"), sem("pool_chunk_made")
        s_cst, s_pm0, s_zero = sem("constants_made"), sem("pool_memsets"), sem("zeros_made")
        s_bq = sem("scaled_biases")
        s_sort, s_sp = sem("sort_step"), sem("sort_products")
        s_order = sem("order_ready")
        s_x = [sem("x_even_loaded"), sem("x_odd_loaded")]
        s_st = [sem("x1_even_stored"), sem("x1_odd_stored")]
        s_out = [sem("out_even_stored"), sem("out_odd_stored")]
        s_wc = [sem(f"mix{n}_loaded") for n in range(4)]
        s_xh, s_xl = sem("x_hi"), sem("x_lo")
        s_z, s_zh, s_zl = sem("z_done"), sem("z_hi"), sem("z_lo")
        s_wch, s_wcl = sem("mix_hi"), sem("mix_lo")
        s_qk, s_qkh, s_qkl = sem("qk_done"), sem("qk_hi"), sem("qk_lo")
        s_s, s_sm, s_e, s_r, s_p = sem("scores_done"), sem("scores_masked"), sem("exp_done"), sem("sum_inverted"), sem("probs_ready")
        s_t, s_pth, s_ptl = sem("probs_transposed"), sem("pt_hi"), sem("pt_lo")
        s_u, s_uh, s_ul = sem("u_done"), sem("u_hi"), sem("u_lo")
        s_o, s_oh, s_ol = sem("o_done"), sem("o_hi"), sem("o_lo")
        s_f, s_ft, s_res = sem("out_chunk_done"), sem("out_chunk_biased"), sem("out_chunk_residual")
        s_turn_sp, s_turn_dve, s_turn_pool = sem("sp_turns"), sem("dve_turns"), sem("pool_turns")
        s_c2, s_tt, s_yf, s_yh, s_yl = sem("y_set_done"), sem("y_hilo_copied"), sem("y_summed"), sem("y_hi"), sem("y_lo")
        s_g, s_gt, s_gs = sem("gate_done"), sem("gate_hilo_copied"), sem("gate_summed")
        s_chain, s_dd, s_ee, s_m = sem("gating_step"), sem("gate_shifted"), sem("gate_exp"), sem("middle_ready")
        s_mt, s_mT = sem("middle_transposed"), sem("middle_copied")

        chunks = []
        for k in range(K):
            chunks.append((wqkv_in[:, k * NQ:(k + 1) * NQ], NQ, wq_h[:, k, :], wq_l[:, k, :], None))
        for k in range(2):
            chunks.append((wo_in[:, k * T:(k + 1) * T], T, wo_h[:, k, :], wo_l[:, k, :], None))
        chunks.append((ag_in, K * RG, ag[:, :, 0:RG], ag[:, :, RG:2 * RG], K))
        chunks.append((bl_in, T, bl_h[:, :], bl_l[:, :], None))
        NCH = len(chunks)
        assert NCH % STAGE == 0 and K % STAGE == 0

        def group_cols(g, lo=0, n=GR):
            return xr[:, bass.ds((g % RING) * GR + lo, n)]

        def batch_view(i, q, b):
            v = group_cols(2 * i + q // 2, (q % 2) * PT2 + b * BT, BT)
            return v.rearrange("p (k s) -> p k s", k=K)

        def split_view(q, b, half):
            return xs[:, q % 2, :, half * P + b * S:half * P + (b + 1) * S]

        def chunk_view(g, m):
            return group_cols(g).rearrange("p (b k s) -> p b k s", b=4, k=K)[:, :, m, :]

        def x_ready(eng, i, q, phase_b):
            u = (q // 2) % 2
            n = q // 4
            if phase_b:
                wait(eng, s_x[u], i, 64, 16 * IA + 64 * (n + 1))
            else:
                wait(eng, s_x[u], i, 16, 16 * (n + 1))

        block = ctx.enter_context(nc.Block())

        @block.sync
        def _(sp):
            def load_x(i, u):
                sp.dma_start(group_cols(2 * i + u), x_in[bass.ds(2 * i + u, 1), :, :].rearrange("a p n -> (a p) n")
                             ).then_inc(s_x[u], 16)

            def load_mix(i, q):
                n = q % 4
                wait(sp, s_wcl, i, 4, q - 3)
                sp.sem_inc(s_turn_sp, 1)
                for b in range(2):
                    e = sp.value_load(idr_i[0:1, bass.ds(8 * i + 2 * q + b, 1)], min_val=0, max_val=NC - 1)
                    dst = wcf[b * S:(b + 1) * S, n, :].rearrange("p (t d) -> p t d", t=2)[:, :, b * S:(b + 1) * S]
                    src = wc_in[bass.ds(e, 1), :, :, :].rearrange("a c t d -> (a c) t d")
                    sp.dma_start(dst, src).then_inc(s_wc[n], 16)

            def load_chunk(n):
                src, w = chunks[n][0], chunks[n][1]
                if n >= STAGE:
                    sp.wait_ge(s_wl, n - STAGE + 1)
                sp.dma_start(stage[:, n % STAGE, 0:w], src).then_inc(s_stage[n % STAGE], 16)

            def store_x1(i, u):
                wait(sp, s_res, i, 16, 8 * (u + 1))
                sp.sem_inc(s_turn_sp, 1)
                sp.dma_start(x1[bass.ds(4 * (2 * i + u), 4), :, :].rearrange("b p n -> p b n"),
                             group_cols(2 * i + u).rearrange("p (b n) -> p b n", b=4)).then_inc(s_st[u], 16)

            sp.dma_start(idr_i[:, :], ids_in.to_broadcast([P, NB])).then_inc(s_ids, 16)
            sp.dma_start(idc_i[0:NB, :], ids_in.rearrange("a b -> b a")).then_inc(s_ids, 16)
            load_x(0, 0)
            load_chunk(0)
            load_chunk(1)
            sp.dma_start(bias[:, :], bias_in).then_inc(s_small, 16)
            for h in range(2):
                sp.dma_start(gb[:, h, :], gb_in.to_broadcast([P, G4])).then_inc(s_small, 16)
            load_chunk(2)
            load_chunk(3)
            sp.wait_ge(s_ids, 32)
            sp.wait_ge(s_zero, 1)
            load_mix(0, 0)
            load_mix(0, 1)
            for n in range(STAGE, NCH):
                load_chunk(n)
                if n == STAGE:
                    load_x(0, 1)

            def body(i, first=False, last=False):
                for u in range(2):
                    if not last:
                        wait(sp, s_st[u], i, 16, 0)
                        sp.sem_inc(s_turn_sp, 1)
                        wait(sp, s_x[u], i, 16, 16)
                        sp.sem_inc(s_turn_sp, 1)
                        load_x(i + 1, u)
                    for j in range(2):
                        q = 2 * u + j
                        if not (last and q >= 2):
                            load_mix(i, q + 2)
                    if u == 1:
                        store_x1(i, 0)
                    elif not first:
                        store_x1(i - 1, 1)

            body(0, first=True)
            with sp.Fori(1, IA - 1) as i:
                body(i)
            body(IA - 1, last=True)
            store_x1(IA - 1, 1)

            def load_slots(i, u):
                for b in range(4):
                    r = sp.value_load(order[0:1, bass.ds(SRC + 4 * (2 * i + u) + b, 1)], min_val=0, max_val=NB - 1)
                    sp.dma_start(group_cols(2 * i + u, b * BT, BT),
                                 x1[bass.ds(r, 1), :, :].rearrange("a p n -> (a p) n")).then_inc(s_x[u], 16)

            def store_out(i, u):
                wait(sp, s_res, i, 16, FA + 8 * (u + 1))
                sp.sem_inc(s_turn_sp, 1)
                for b in range(4):
                    r = sp.value_load(order[0:1, bass.ds(DST + 4 * (2 * i + u) + b, 1)], min_val=0, max_val=NB + NC - 1)
                    sp.dma_start(out[bass.ds(r, 1), :, :].rearrange("a p n -> (a p) n"),
                                 group_cols(2 * i + u, b * BT, BT)).then_inc(s_out[u], 16)

            for u in range(2):
                sp.wait_ge(s_st[u], 16 * IA)
            sp.wait_ge(s_order, 1)
            for u in range(2):
                load_slots(0, u)

            def body_b(i, first=False, last=False):
                for u in range(2):
                    if not last:
                        wait(sp, s_out[u], i, 64, 0)
                        sp.sem_inc(s_turn_sp, 1)
                        wait(sp, s_x[u], i, 64, 16 * IA + 64)
                        sp.sem_inc(s_turn_sp, 1)
                        load_slots(i + 1, u)
                    if u == 1:
                        store_out(i, 0)
                    elif not first:
                        store_out(i - 1, 1)

            body_b(0, first=True)
            with sp.Fori(1, IB - 1) as i:
                body_b(i)
            body_b(IB - 1, last=True)
            store_out(IB - 1, 1)
            for u in range(2):
                sp.wait_ge(s_out[u], 64 * IB)

        @block.gpsimd
        def _(pool):
            pool.memset(ident[:, :], 0.0).then_inc(s_pm0, 1)
            pool.memset(ones[:, :], 1.0).then_inc(s_pm0, 1)
            pool.memset(cols[:, 1:2], 1.0).then_inc(s_pm0, 1)
            pool.iota(cols[:, 0:1], pattern=[[0, 1]], base=0, channel_multiplier=1,
                      allow_small_or_imprecise_dtypes=True).then_inc(s_cst, 1)
            pool.iota(iota_e[:, :], pattern=[[1, NC]], base=0, channel_multiplier=0,
                      allow_small_or_imprecise_dtypes=True).then_inc(s_cst, 1)
            pool.iota(iota_s[:, :], pattern=[[1, SLOT]], base=0, channel_multiplier=0,
                      allow_small_or_imprecise_dtypes=True).then_inc(s_cst, 1)
            pool.iota(spare[:, :], pattern=[[0, SLOT // NC], [1, NC]], base=NB, channel_multiplier=0,
                      allow_small_or_imprecise_dtypes=True).then_inc(s_cst, 1)
            pool.wait_ge(s_pm0, 3)
            pool.affine_select(out=lower[:, :], in_=ones[:, 0:NB], compare_op=ALU.is_gt, fill=0.0, base=0,
                               pattern=[[-1, NB]], channel_multiplier=1).then_inc(s_cst, 1)
            pool.wait_ge(s_cst, 5)
            pool.affine_select(out=tri[:, 0:NC], in_=ones[0:NC, 0:NC], compare_op=ALU.is_gt, fill=0.0, base=0,
                               pattern=[[1, NC]], channel_multiplier=-1).then_inc(s_cst, 1)
            pool.wait_ge(s_cst, 6)
            pool.affine_select(out=tri[:, NC:2 * NC], in_=ones[0:NC, 0:NC], compare_op=ALU.is_ge, fill=0.0, base=0,
                               pattern=[[1, NC]], channel_multiplier=-1).then_inc(s_cst, 1)
            pool.wait_ge(s_cst, 7)
            pool.affine_select(out=ident[:, :], in_=ident[:, :], compare_op=ALU.not_equal, fill=1.0, base=0,
                               pattern=[[-1, P]], channel_multiplier=1).then_inc(s_cst, 1)
            pool.wait_ge(s_cst, 8)
            pool.tensor_copy(ident16[:, :], ident[:, :]).then_inc(s_cst, 1)

            def load(src, st):
                pool.dma_start(stage[:, st, :], src).then_inc(s_pst[st], 16)

            def convert(hi, lo, st, seen, done):
                pool.wait_ge(s_pst[st], 16 * seen + 16)
                pool.sem_inc(s_turn_pool, 1)
                pool.tensor_scalar(hi, stage[:, st, :], SW, 1.0, ALU.mult, ALU.mult).then_inc(s_pc, 1)
                pool.tensor_scalar(stage[:, st, :], stage[:, st, :], SW, 1.0, ALU.mult, ALU.mult).then_inc(s_pc, 1)
                pool.wait_ge(s_pc, 2 * done + 2)
                pool.tensor_tensor(lo, stage[:, st, :], hi, ALU.subtract).then_inc(s_pw, 1)

            pool.wait_ge(s_wl, NCH)
            for k in range(STAGE):
                load(w_in[:, k * T:(k + 1) * T], k)
            for k in range(K):
                convert(wf_h[:, k, :], wf_l[:, k, :], k % STAGE, k // STAGE, k)
                pool.wait_ge(s_pw, k + 1)
                if k + STAGE < K:
                    load(w_in[:, (k + STAGE) * T:(k + STAGE + 1) * T], k % STAGE)
            for k in range(STAGE):
                load(w2_in[0, :, k * T:(k + 1) * T], k)

            def condition(i, b, more=True):
                hi = w2[:, b, 0:K * T].rearrange("p (k n) -> p k n", k=K)
                lo = w2[:, b, K * T:].rearrange("p (k n) -> p k n", k=K)
                e = 2 * i + b
                for k in range(K):
                    convert(hi[:, k, :], lo[:, k, :], k % STAGE, (K + K * e + k) // STAGE if isinstance(e, int) else K // STAGE * (e + 1) + k // STAGE,
                            K + K * e + k)
                    pool.wait_ge(s_pw, K * e + K + k + 1)
                    if k < K - STAGE:
                        load(w2_in[bass.ds(e, 1), :, (k + STAGE) * T:(k + STAGE + 1) * T].rearrange("a p n -> (a p) n"), k % STAGE)
                    elif more:
                        kk = k - (K - STAGE)
                        load(w2_in[bass.ds(e + 1, 1), :, kk * T:(kk + 1) * T].rearrange("a p n -> (a p) n"), k % STAGE)

            condition(0, 0)
            pool.wait_ge(s_f, FA)
            condition(0, 1)
            pool.wait_ge(s_order, 1)

            def free_buffer(i, b):
                n = pool.value_load(order[0:1, bass.ds(CUM + 2 * i + b - 2, 1)], min_val=0, max_val=NSL)
                pool.wait_ge(s_c2, 4 * n + 1)

            with pool.Fori(1, NC // 2 - 1) as i:
                for b in range(2):
                    free_buffer(i, b)
                    condition(i, b)
            i = NC // 2 - 1
            free_buffer(i, 0)
            condition(i, 0)
            free_buffer(i, 1)
            condition(i, 1, more=False)

        @block.scalar
        def _(act):
            Copy, Iden = ACT.Copy, ACT.Identity

            act.wait_ge(s_small, 48)
            nc.scalar.activation(biasq[:, 0:4], bias[:, B_QK:B_QK + 4], Copy, scale=SQ).then_inc(s_bq, 1)
            nc.scalar.activation(biasq[:, 4:6], bias[:, B_V:B_V + 2], Copy, scale=SO).then_inc(s_bq, 1)

            def x_hi(i, q, phase_b=False):
                x_ready(act, i, q, phase_b)
                for b in range(2):
                    last = nc.scalar.activation(split_view(q, b, 0), batch_view(i, q, b), Copy, scale=SX)
                last.then_inc(s_xh, 1)

            def mix_hi(i, q):
                wait(act, s_wc[q % 4], i, 32, 32 * (q // 4 + 1))
                wait(act, s_u, i, 4, q - 1)
                nc.scalar.activation(wch[:, q % 2, :], wcf[:, q % 4, :], Copy, scale=SC).then_inc(s_wch, 1)

            x_hi(0, 0)
            for n, (_, w, hi, _, k) in enumerate(chunks):
                act.wait_ge(s_stage[n % STAGE], 16 * (n // STAGE + 1))
                src = stage[:, n % STAGE, 0:w]
                if k:
                    src = src.rearrange("p (k n) -> p k n", k=k)
                nc.scalar.activation(hi, src, Copy, scale=SW).then_inc(s_wh, 1)
                if n == 3:
                    mix_hi(0, 0)
                if n == 7:
                    x_hi(0, 1)

            def out_chunks(i, u, ms, n0, scale, b0):
                for m in ms:
                    wait(act, s_f, i, 16, n0 + 8 * u + m + 1)
                    wait(act, s_res, i, 16, n0 + 8 * u + m - 1)
                    src = (wops if n0 == 0 else fps)[m % 2]
                    nc.scalar.activation(ft[:, m % 2, :], src[:, 0:2 * P], Iden, bias=bias[:, b0 + m:b0 + m + 1],
                                         scale=scale).then_inc(s_ft, 1)

            def a_step(i, q, last=False):
                u, j = q // 2, q % 2
                wait(act, s_z, i, 4, q + 1)
                for h in range(2):
                    e = nc.scalar.activation(zh[:, q % 2, h * 384:(h + 1) * 384], zps[q % 2][h][:, 0:384], Copy,
                                             scale=SZ / (SX * SW))
                e.then_inc(s_zh, 1)
                if j == 0:
                    if u == 1:
                        out_chunks(i, 0, range(K), 0, 1.0 / (SO * SW), B_O)
                    elif not (isinstance(i, int) and i == 0):
                        out_chunks(i - 1, 1, range(K), 0, 1.0 / (SO * SW), B_O)
                wait(act, s_qk, i, 4, q + 1)
                for c in range(4):
                    e = nc.scalar.activation(qkh[:, c, :], qkps[:, c * P:(c + 1) * P], Iden, bias=biasq[:, c:c + 1])
                e.then_inc(s_qkh, 1)
                if not (last and q == 3):
                    mix_hi(i, q + 1)
                wait(act, s_sm, i, 4, q + 1)
                nc.scalar.activation(ex[:, :], sm[:, :], ACT.Exp, bias=soft[:, 0:1], scale=-1.0,
                                     accum_out=soft[:, 1:2]).then_inc(s_e, 1)
                if not (last and q >= 2):
                    x_hi(i, q + 2)
                wait(act, s_t, i, 4, q + 1)
                nc.scalar.copy(pth[:, :], chps[:, 0:P]).then_inc(s_pth, 1)
                wait(act, s_u, i, 4, q + 1)
                nc.scalar.activation(uh[:, :], chps[:, 0:P], Copy, scale=SU / (SC * SP)).then_inc(s_uh, 1)
                wait(act, s_o, i, 4, q + 1)
                for c in range(2):
                    e = nc.scalar.activation(oh[:, u, c, j * P:(j + 1) * P], chps[:, c * P:(c + 1) * P], Iden,
                                             bias=biasq[:, 4 + c:5 + c])
                e.then_inc(s_oh, 1)

            def a_body(i, last=False):
                for q in range(4):
                    a_step(i, q, last)

            act.wait_ge(s_bq, 2)
            a_body(0)
            with act.Fori(1, IA - 1) as i:
                a_body(i)
            a_body(IA - 1, last=True)
            out_chunks(IA - 1, 1, range(K), 0, 1.0 / (SO * SW), B_O)

            def y_set(i, q, t):
                wait(act, s_c2, i, 16, 4 * q + t + 2)
                wait(act, s_yf, i, 16, 4 * q + t - 1)
                src = c2ps[t][:, :].rearrange("p (m h n) -> p m h n", m=2, h=2)
                nc.scalar.activation(tt[:, t % 2, :, :], src[:, :, 1, :], Copy, scale=1.0 / SW).then_inc(s_tt, 1)
                wait(act, s_yf, i, 16, 4 * q + t + 1)
                nc.scalar.copy(yh[:, q // 2, 2 * t:2 * t + 2, (q % 2) * P:(q % 2 + 1) * P], yf[:, t % 2, :, :]).then_inc(s_yh, 1)

            def gate_copy(i, q):
                wait(act, s_g, i, 4, q + 1)
                wait(act, s_gs, i, 4, q)
                nc.scalar.copy(gt[:, :], gps[:, RG:2 * RG]).then_inc(s_gt, 1)

            def gate_exp(i, u):
                wait(act, s_dd, i, 2, u + 1)
                nc.scalar.activation(ee[:, :, :], dd[:, :, :], ACT.Exp).then_inc(s_ee, 1)

            def middle_copy(i, u):
                wait(act, s_mt, i, 2, u + 1)
                nc.scalar.copy(mT[:, :], mtps).then_inc(s_mT, 1)

            def b_step(i, q, first=False, last=False):
                u, j = q // 2, q % 2
                pi, pu = (i, 0) if u == 1 else (i - 1, 1)
                y_set(i, q, 0)
                if q > 0:
                    gate_copy(i, q - 1)
                elif not first:
                    gate_copy(i - 1, 3)
                before = not (first and u == 0)
                if j == 0 and before:
                    gate_exp(pi, pu)
                y_set(i, q, 1)
                if not (last and q == 3):
                    x_hi(i, q + 1, phase_b=True)
                y_set(i, q, 2)
                if j == 0 and before:
                    middle_copy(pi, pu)
                y_set(i, q, 3)
                if before:
                    out_chunks(pi, pu, range(4 * j, 4 * j + 4), FA, 1.0 / (SX * SW), B_F)

            def b_body(i, first=False, last=False):
                for q in range(4):
                    b_step(i, q, first, last)

            x_hi(0, 0, phase_b=True)
            b_body(0, first=True)
            with act.Fori(1, IB - 1) as i:
                b_body(i)
            b_body(IB - 1, last=True)
            gate_copy(IB - 1, 3)
            gate_exp(IB - 1, 1)
            middle_copy(IB - 1, 1)
            out_chunks(IB - 1, 1, range(K), FA, 1.0 / (SX * SW), B_F)

        @block.vector
        def _(dve):
            v = nc.vector
            v.memset(wcf[:, :, :], 0.0).then_inc(s_zero, 1)
            for a in range(2):
                for b in range(2):
                    v.memset(mask[a * S:(a + 1) * S, b * S:(b + 1) * S], 0.0 if a == b else MASKED).then_inc(s_zero, 1)

            done = [0]

            def link(ins):
                done[0] += 1
                ins.then_inc(s_sort, 1)
                dve.wait_ge(s_sort, done[0])

            dve.wait_ge(s_ids, 32)
            dve.wait_ge(s_cst, 9)
            dve.wait_ge(s_zero, 5)
            link(v.tensor_copy(cols[0:NB, 2:3], idc_i[0:NB, :]))
            link(v.tensor_copy(idr[0:NB, :], idr_i[0:NB, :]))
            link(v.tensor_scalar(idr[0:NB, :], idr[0:NB, :], cols[0:NB, 2:3], None, ALU.is_equal))
            link(v.tensor_tensor_reduce(out=idr[0:NB, :], in0=idr[0:NB, :], in1=lower[0:NB, :], scale=1.0, scalar=0.0,
                                        op0=ALU.mult, op1=ALU.add, accum_out=rank[0:NB, 0:1]))
            link(v.tensor_scalar(hot[0:NB, 0:NC], iota_e[0:NB, :], cols[0:NB, 2:3], None, ALU.is_equal))
            dve.wait_ge(s_sp, 1)
            link(v.tensor_copy(cnt_i[:, 0:1], trps[0:NC, 0:1]))
            link(v.tensor_copy(cnt[:, 0:1], trps[0:NC, 0:1]))
            link(v.tensor_scalar(cnt_i[:, 1:2], cnt_i[:, 0:1], 1, None, ALU.bitwise_and))
            link(v.tensor_copy(cnt[:, 1:2], cnt_i[:, 1:2]))
            link(v.tensor_tensor(cnt[:, 2:3], cnt[:, 0:1], cnt[:, 1:2], ALU.add))
            link(v.tensor_scalar(pcb[:, :], ones[0:NC, :], cnt[:, 2:3], 0.5, ALU.mult, ALU.mult))
            dve.wait_ge(s_sp, 2)
            link(v.tensor_tensor_reduce(out=hot[0:NB, 0:NC], in0=hot[0:NB, 0:NC], in1=trps[0:NB, 0:NC], scale=2.0,
                                        scalar=0.0, op0=ALU.mult, op1=ALU.add, accum_out=rank[0:NB, 1:2]))
            link(v.tensor_copy(order[0:1, CUM:CUM + NC], trps[0:1, NC:2 * NC]))
            link(v.tensor_tensor(rank[0:NB, 2:3], rank[0:NB, 0:1], rank[0:NB, 1:2], ALU.add))
            link(v.tensor_scalar(hot[0:NB, :], iota_s[0:NB, :], rank[0:NB, 2:3], None, ALU.is_equal))
            dve.wait_ge(s_sp, 3)
            link(v.tensor_copy(rows[:, 0:3 * SLOT], trps[0:1, 0:3 * SLOT]))
            link(v.tensor_copy(order[0:1, SRC:SRC + SLOT], rows[:, 0:SLOT]))
            link(v.scalar_tensor_tensor(out=rows[:, 3 * SLOT:4 * SLOT], in0=rows[:, SLOT:2 * SLOT], scalar=-1.0,
                                        in1=spare[:, :], op0=ALU.add, op1=ALU.mult))
            link(v.tensor_tensor(order[0:1, DST:DST + SLOT], rows[:, 0:SLOT], rows[:, 3 * SLOT:4 * SLOT],
                                 ALU.subtract))
            link(v.scalar_tensor_tensor(out=rows[:, 4 * SLOT:5 * SLOT], in0=rows[:, SLOT:2 * SLOT],
                                        scalar=-float(NC - 1), in1=rows[:, 2 * SLOT:3 * SLOT], op0=ALU.mult,
                                        op1=ALU.add))
            v.tensor_scalar(order[0:1, CND:CND + SLOT], rows[:, 4 * SLOT:5 * SLOT], float(NC - 1), None,
                            ALU.add).then_inc(s_order, 1)

            def x_lo(i, q, b, phase_b=False):
                x_ready(dve, i, q, phase_b)
                wait(dve, s_xh, i, 4, (NP if phase_b else 0) + q + 1)
                e = v.scalar_tensor_tensor(out=split_view(q, b, 1), in0=batch_view(i, q, b), scalar=SX,
                                           in1=split_view(q, b, 0), op0=ALU.mult, op1=ALU.subtract)
                if b == 1:
                    e.then_inc(s_xl, 1)

            def mix_lo(i, q):
                wait(dve, s_wch, i, 4, q + 1)
                v.scalar_tensor_tensor(out=wcl[:, q % 2, :], in0=wcf[:, q % 4, :], scalar=SC, in1=wch[:, q % 2, :],
                                       op0=ALU.mult, op1=ALU.subtract).then_inc(s_wcl, 1)

            for b in range(2):
                x_lo(0, 0, b)
            for n, (_, w, hi, lo, k) in enumerate(chunks):
                dve.wait_ge(s_wh, n + 1)
                src = stage[:, n % STAGE, 0:w]
                if k:
                    src = src.rearrange("p (k n) -> p k n", k=k)
                v.scalar_tensor_tensor(out=lo, in0=src, scalar=SW, in1=hi, op0=ALU.mult,
                                       op1=ALU.subtract).then_inc(s_wl, 1)
                if n == 3:
                    mix_lo(0, 0)
                if n == 7:
                    for b in range(2):
                        x_lo(0, 1, b)

            def residual(i, u, ms, n0):
                for m in ms:
                    wait(dve, s_ft, i, 16, n0 + 8 * u + m + 1)
                    ring = chunk_view(2 * i + u, m)
                    v.tensor_tensor(ring, ft[:, m % 2, :].rearrange("p (b s) -> p b s", b=4), ring,
                                    ALU.add).then_inc(s_res, 1)

            def a_step(i, q, last=False):
                u, j = q // 2, q % 2
                wait(dve, s_zh, i, 4, q + 1)
                for h in range(2):
                    c = slice(h * 384, (h + 1) * 384)
                    e = v.scalar_tensor_tensor(out=zl[:, q % 2, c], in0=zps[q % 2][h][:, 0:384],
                                               scalar=SZ / (SX * SW), in1=zh[:, q % 2, c], op0=ALU.mult,
                                               op1=ALU.subtract)
                e.then_inc(s_zl, 1)
                if j == 0:
                    if u == 1:
                        residual(i, 0, range(K), 0)
                    elif not (isinstance(i, int) and i == 0):
                        residual(i - 1, 1, range(K), 0)
                wait(dve, s_qkh, i, 4, q + 1)
                for c in range(4):
                    e = v.scalar_tensor_tensor(out=qkl[:, c, :], in0=qkps[:, c * P:(c + 1) * P],
                                               scalar=biasq[:, c:c + 1], in1=qkh[:, c, :], op0=ALU.add,
                                               op1=ALU.subtract)
                e.then_inc(s_qkl, 1)
                if not (last and q == 3):
                    mix_lo(i, q + 1)
                wait(dve, s_s, i, 4, q + 1)
                dve.sem_inc(s_turn_dve, 1)
                v.tensor_tensor_reduce(out=sm[:, :], in0=chps[:, 0:P], in1=mask[:, :], scale=-EXP_SCALE,
                                       scalar=3.0e38, op0=ALU.add, op1=ALU.min,
                                       accum_out=soft[:, 0:1]).then_inc(s_sm, 1)
                wait(dve, s_e, i, 4, q + 1)
                v.reciprocal(soft[:, 2:3], soft[:, 1:2]).then_inc(s_r, 1)
                wait(dve, s_r, i, 4, q + 1)
                v.tensor_scalar(pn[:, :], ex[:, :], soft[:, 2:3], SP, ALU.mult, ALU.mult).then_inc(s_p, 1)
                if not (last and q >= 2):
                    x_lo(i, q + 2, 0)
                wait(dve, s_pth, i, 4, q + 1)
                v.tensor_tensor(ptl[:, :], chps[:, 0:P], pth[:, :], ALU.subtract).then_inc(s_ptl, 1)
                wait(dve, s_uh, i, 4, q + 1)
                v.scalar_tensor_tensor(out=ul[:, :], in0=chps[:, 0:P], scalar=SU / (SC * SP), in1=uh[:, :],
                                       op0=ALU.mult, op1=ALU.subtract).then_inc(s_ul, 1)
                if not (last and q >= 2):
                    x_lo(i, q + 2, 1)
                wait(dve, s_oh, i, 4, q + 1)
                for c in range(2):
                    e = v.scalar_tensor_tensor(out=ol[:, u, c, j * P:(j + 1) * P], in0=chps[:, c * P:(c + 1) * P],
                                               scalar=biasq[:, 4 + c:5 + c], in1=oh[:, u, c, j * P:(j + 1) * P],
                                               op0=ALU.add, op1=ALU.subtract)
                e.then_inc(s_ol, 1)

            def a_body(i, last=False):
                for q in range(4):
                    a_step(i, q, last)

            a_body(0)
            with dve.Fori(1, IA - 1) as i:
                a_body(i)
            a_body(IA - 1, last=True)
            residual(IA - 1, 1, range(K), 0)

            def y_set(i, q, t):
                wait(dve, s_yl, i, 16, 4 * q + t - 1)
                wait(dve, s_tt, i, 16, 4 * q + t + 1)
                src = c2ps[t][:, :].rearrange("p (m h n) -> p m h n", m=2, h=2)
                v.scalar_tensor_tensor(out=yf[:, t % 2, :, :], in0=src[:, :, 0, :], scalar=1.0 / SW, in1=tt[:, t % 2, :, :],
                                       op0=ALU.mult, op1=ALU.add).then_inc(s_yf, 1)
                wait(dve, s_yh, i, 16, 4 * q + t + 1)
                c = slice((q % 2) * P, (q % 2 + 1) * P)
                v.tensor_tensor(yl[:, q // 2, 2 * t:2 * t + 2, c], yf[:, t % 2, :, :], yh[:, q // 2, 2 * t:2 * t + 2, c],
                                ALU.subtract).then_inc(s_yl, 1)

            def gate_sum(i, q):
                wait(dve, s_gt, i, 4, q + 1)
                v.tensor_tensor(gs[:, q % 2, :], gps[:, 0:RG], gt[:, :], ALU.add).then_inc(s_gs, 1)

            STEPS = 12

            def gating(i, u, part):
                n = [0 if part == 1 else 5]

                def link(ins):
                    n[0] += 1
                    ins.then_inc(s_chain, 1)
                    wait(dve, s_chain, i, 2 * STEPS, u * STEPS + n[0])

                if part == 1:
                    wait(dve, s_gs, i, 4, 2 * u + 2)
                    link(v.scalar_tensor_tensor(out=sc[:, :, :], in0=gs[:, :, R:RG], scalar=1.0 / (SX * SW),
                                                in1=gb[:, :, :], op0=ALU.mult, op1=ALU.add))
                    pairs = sc[:, :, :].rearrange("p h (a b) -> p h a b", b=2)
                    link(v.tensor_tensor(pm[:, :, :], pairs[:, :, :, 0], pairs[:, :, :, 1], ALU.max))
                    link(v.tensor_tensor(m012[:, :, :], pm[:, :, 0:1], sc[:, :, 2:3], ALU.max))
                    link(v.tensor_tensor(m123[:, :, :], pm[:, :, 1:2], sc[:, :, 1:2], ALU.max))
                    link(v.tensor_tensor(mx[:, :, :], pm[:, :, 0:1], pm[:, :, 1:2], ALU.max))
                    v.tensor_tensor(dd[:, :, :], sc[:, :, :], mx[:, :, :].to_broadcast([P, 2, G4]),
                                    ALU.subtract).then_inc(s_dd, 1)
                    return
                wait(dve, s_ee, i, 2, u + 1)
                link(v.reduce_sum(den[:, :], ee[:, :, :], axis=AX.X))
                link(v.reciprocal(ptop[:, :], den[:, :]))
                link(v.reciprocal(itop[:, :], ptop[:, :]))
                w = cw[:, :, 0:1]
                link(v.tensor_tensor(w, ptop[:, :].rearrange("p (h a) -> p h a", a=1),
                                     itop[:, :].rearrange("p (h a) -> p h a", a=1), ALU.mult))
                v.tensor_tensor(cw[:, :, 1:2], m123[:, :, :], sc[:, :, 0:1], ALU.is_gt)
                v.tensor_tensor(cw[:, :, 2:3], pm[:, :, 1:2], pm[:, :, 0:1], ALU.is_gt)
                link(v.tensor_tensor(cw[:, :, 3:4], sc[:, :, 3:4], m012[:, :, :], ALU.is_gt))
                lo = 0
                for r, hi in enumerate(RANKS):
                    n_c = hi - lo
                    f = cw[:, :, r:r + 1].to_broadcast([P, 2, n_c])
                    e = v.scalar_tensor_tensor(out=mf[:, :, lo:hi], in0=gs[:, :, lo:hi], scalar=1.0 / SW, in1=f,
                                               op0=ALU.mult, op1=ALU.mult)
                    lo = hi
                link(e)
                v.tensor_tensor(mf[:, :, RANKS[0]:R], mf[:, :, RANKS[0]:R],
                                w.to_broadcast([P, 2, R - RANKS[0]]), ALU.mult).then_inc(s_chain, 1)
                wait(dve, s_chain, i, 2 * STEPS, (u + 1) * STEPS)
                v.tensor_copy(mhl[:, :, 0:R], mf[:, :, :]).then_inc(s_m, 1)
                wait(dve, s_m, i, 4, 2 * u + 1)
                v.tensor_tensor(mhl[:, :, R:2 * R], mf[:, :, :], mhl[:, :, 0:R], ALU.subtract).then_inc(s_m, 1)

            def b_step(i, q, first=False, last=False):
                u, j = q // 2, q % 2
                pi, pu = (i, 0) if u == 1 else (i - 1, 1)
                before = not (first and u == 0)
                y_set(i, q, 0)
                if q > 0:
                    gate_sum(i, q - 1)
                elif not first:
                    gate_sum(i - 1, 3)
                if j == 0 and before:
                    gating(pi, pu, 1)
                y_set(i, q, 1)
                if j == 0 and before:
                    gating(pi, pu, 2)
                if not (last and q == 3):
                    for b in range(2):
                        x_lo(i, q + 1, b, phase_b=True)
                y_set(i, q, 2)
                y_set(i, q, 3)
                if before:
                    residual(pi, pu, range(4 * j, 4 * j + 4), FA)

            def b_body(i, first=False, last=False):
                for q in range(4):
                    b_step(i, q, first, last)

            for b in range(2):
                x_lo(0, 0, b, phase_b=True)
            b_body(0, first=True)
            with dve.Fori(1, IB - 1) as i:
                b_body(i)
            b_body(IB - 1, last=True)
            gate_sum(IB - 1, 3)
            gating(IB - 1, 1, 1)
            gating(IB - 1, 1, 2)
            residual(IB - 1, 1, range(K), FA)

        @block.tensor
        def _(pe):
            mm = nc.tensor.matmul

            def three(dst, pairs, first=True, last=True):
                n = len(pairs)
                for k, (ah, al, bh, bl) in enumerate(pairs):
                    mm(dst, ah, bh, start=first and k == 0, stop=False)
                    mm(dst, ah, bl, start=False, stop=False)
                    e = mm(dst, al, bh, start=False, stop=last and k == n - 1)
                return e

            pe.wait_ge(s_cst, 9)
            pe.wait_ge(s_sort, 5)
            mm(trps[0:NC, 0:1], hot[0:NB, 0:NC], ones[0:NB, 0:1], start=True, stop=True).then_inc(s_sp, 1)
            pe.wait_ge(s_sort, 11)
            mm(trps[:, 0:2 * NC], pcb[:, :], tri[:, :], start=True, stop=True).then_inc(s_sp, 1)
            pe.wait_ge(s_sort, 15)
            for r in range(3):
                e = mm(trps[0:1, r * SLOT:(r + 1) * SLOT], cols[0:NB, r:r + 1], hot[0:NB, :], start=True, stop=True)
            e.then_inc(s_sp, 1)

            def z_part(i, q, ks, start_up=False):
                if ks[0] == 0:
                    wait(pe, s_xl, i, 4, q + 1)
                    wait(pe, s_zl, i, 4, q - 1)
                for k in ks:
                    if start_up:
                        pe.wait_ge(s_wl, k + 1)
                    a, b = xs[:, q % 2, k, 0:P], xs[:, q % 2, k, P:2 * P]
                    for lhs, rhs in ((a, wq_h), (a, wq_l), (b, wq_h)):
                        for h in range(2):
                            e = mm(zps[q % 2][h][:, 0:384], lhs, rhs[:, k, h * 384:(h + 1) * 384],
                                   start=(k == 0 and lhs is a and rhs is wq_h),
                                   stop=(k == K - 1 and lhs is b))
                if ks[-1] == K - 1:
                    e.then_inc(s_z, 1)

            def out_products(i, u):
                wait(pe, s_ol, i, 4, 2 * u + 2)
                for m in range(K):
                    wait(pe, s_ft, i, 16, 8 * u + m - 1)
                    c = slice(m * P, (m + 1) * P)
                    three(wops[m % 2][:, 0:2 * P],
                          [(wo_h[:, d, c], wo_l[:, d, c], oh[:, u, d, :], ol[:, u, d, :]) for d in range(2)]
                          ).then_inc(s_f, 1)

            def a_step(i, q, last=False):
                u, j = q // 2, q % 2
                more = not (last and q == 3)
                zz = (lambda *ks: z_part(i, q + 1, ks)) if more else (lambda *ks: None)
                r = q % 2
                zz(0, 1)
                if j == 0:
                    if u == 1:
                        out_products(i, 0)
                    elif not (isinstance(i, int) and i == 0):
                        out_products(i - 1, 1)
                wait(pe, s_zl, i, 4, q + 1)
                wait(pe, s_wcl, i, 4, q + 1)
                for c in range(4):
                    d = slice(c * P, (c + 1) * P)
                    e = three(qkps[:, d], [(zh[:, r, d], zl[:, r, d], wch[:, r, 0:P], wcl[:, r, 0:P])])
                e.then_inc(s_qk, 1)
                zz(2, 3)
                wait(pe, s_qkl, i, 4, q + 1)
                wait(pe, s_ol, i, 4, q)
                three(chps[:, 0:P], [(qkh[:, c, :], qkl[:, c, :], qkh[:, 2 + c, :], qkl[:, 2 + c, :])
                                     for c in range(2)]).then_inc(s_s, 1)
                zz(4, 5)
                wait(pe, s_p, i, 4, q + 1)
                nc.tensor.transpose(chps[:, 0:P], pn[:, :], ident[:, :]).then_inc(s_t, 1)
                zz(6)
                wait(pe, s_ptl, i, 4, q + 1)
                three(chps[:, 0:P], [(wch[:, r, P:2 * P], wcl[:, r, P:2 * P], pth[:, :], ptl[:, :])]).then_inc(s_u, 1)
                zz(7)
                wait(pe, s_ul, i, 4, q + 1)
                for c in range(2):
                    d = slice(2 * DH + c * P, 2 * DH + (c + 1) * P)
                    e = three(chps[:, c * P:(c + 1) * P], [(zh[:, r, d], zl[:, r, d], uh[:, :], ul[:, :])])
                e.then_inc(s_o, 1)

            def a_body(i, last=False):
                for q in range(4):
                    a_step(i, q, last)

            z_part(0, 0, range(K), start_up=True)
            pe.wait_ge(s_wl, NCH)
            a_body(0)
            with pe.Fori(1, IA - 1) as i:
                a_body(i)
            a_body(IA - 1, last=True)
            out_products(IA - 1, 1)

            def cond_set(i, q, t, b):
                hi = w2[:, b, 0:K * T].rearrange("p (k n) -> p k n", k=K)
                lo = w2[:, b, K * T:].rearrange("p (k n) -> p k n", k=K)
                wait(pe, s_yf, i, 16, 4 * q + t - 3)
                for m in range(2):
                    c = slice((2 * t + m) * P, (2 * t + m + 1) * P)
                    for k in range(K):
                        mm(c2ps[t][:, m * 2 * P:(m + 1) * 2 * P], hi[:, k, c], xs[:, q % 2, k, :], start=(k == 0),
                           stop=False)
                    for k in range(K):
                        e = mm(c2ps[t][:, m * 2 * P:m * 2 * P + P], lo[:, k, c], xs[:, q % 2, k, 0:P], start=False,
                               stop=(k == K - 1))
                e.then_inc(s_c2, 1)

            def gate(i, q):
                u, c = q // 2, slice((q % 2) * P, (q % 2 + 1) * P)
                wait(pe, s_yl, i, 16, 4 * q + 4)
                wait(pe, s_gs, i, 4, q)
                for k in range(K):
                    mm(gps[:, 0:2 * RG], yh[:, u, k, c], ag[:, k, :], start=(k == 0), stop=False)
                for k in range(K):
                    e = mm(gps[:, 0:RG], yl[:, u, k, c], ag[:, k, 0:RG], start=False, stop=(k == K - 1))
                e.then_inc(s_g, 1)

            def transposes(i, u):
                wait(pe, s_m, i, 4, 2 * u + 2)
                for h in range(2):
                    e = nc.tensor.transpose(mtps[:, h * P:(h + 1) * P], mhl[:, h, :], ident16[:, :])
                e.then_inc(s_mt, 1)

            def ffn(i, u, ms):
                for m in ms:
                    wait(pe, s_ft, i, 16, FA + 8 * u + m - 1)
                    c = slice(m * P, (m + 1) * P)
                    dst = fps[m % 2][:, 0:2 * P]
                    three(dst, [(wf_h[:, k, c], wf_l[:, k, c], yh[:, u, k, :], yl[:, u, k, :]) for k in range(K)],
                          last=False)
                    wait(pe, s_mT, i, 2, u + 1)
                    mm(dst, bl_h[:, c], mT[:, :], start=False, stop=False)
                    mm(dst, bl_l[0:R, c], mT[0:R, :], start=False, stop=True).then_inc(s_f, 1)

            def b_step(i, q, first=False):
                u, j = q // 2, q % 2
                pi, pu = (i, 0) if u == 1 else (i - 1, 1)
                before = not (first and u == 0)
                e = pe.value_load(order[0:1, bass.ds(CND + 8 * i + 2 * q, 1)], min_val=0, max_val=NC - 1)
                pe.wait_ge(s_pw, K * e + 2 * K)
                wait(pe, s_xl, i, 4, NP + q + 1)

                def conditioned(b):
                    cond_set(i, q, 0, b)
                    if q > 0:
                        gate(i, q - 1)
                    elif not first:
                        gate(i - 1, 3)
                    cond_set(i, q, 1, b)
                    cond_set(i, q, 2, b)
                    if j == 0 and before:
                        transposes(pi, pu)
                    cond_set(i, q, 3, b)

                with pe.If(e % 2):
                    conditioned(1)
                with pe.Else():
                    conditioned(0)
                if before:
                    ffn(pi, pu, range(4 * j, 4 * j + 4))

            def b_body(i, first=False):
                for q in range(4):
                    b_step(i, q, first)

            pe.wait_ge(s_order, 1)
            pe.wait_ge(s_res, FA)
            pe.wait_ge(s_pw, K)
            pe.sem_inc(s_c2, 1)
            b_body(0, first=True)
            with pe.Fori(1, IB - 1) as i:
                b_body(i)
            b_body(IB - 1)
            gate(IB - 1, 3)
            transposes(IB - 1, 1)
            ffn(IB - 1, 1, range(K))


def kernel(x, itok_B_0_15, L0_cond_weights, L0_attn_Wqkv, L0_attn_bqkv, L0_attn_Wo, L0_attn_bo, L0_cond2_weight,
           L0_ffn_W, L0_ffn_b, L0_ffn_A, L0_ffn_B, L0_ffn_gate_w, L0_ffn_gate_b):
    import numpy as np
    from concourse import bacc
    from concourse.bass_utils import run_bass_kernel_spmd

    a = {n: np.asarray(v) for n, v in locals().items() if n not in ("np", "bacc", "run_bass_kernel_spmd")}
    x = a["x"]
    NB = x.shape[0]

    def chunked(w):
        return np.ascontiguousarray(w.reshape(-1, P, w.shape[1]).transpose(1, 0, 2).reshape(P, -1))

    wc = a["L0_cond_weights"]
    bias = np.concatenate([a[n].reshape(-1, P).T for n in ("L0_attn_bqkv", "L0_attn_bo", "L0_ffn_b")], axis=1)
    bt = a["L0_ffn_B"].T
    arrays = {
        "x_in": x.reshape(NB // 4, 4, S, K, P).transpose(0, 4, 1, 3, 2).reshape(NB // 4, P, GR),
        "ids_in": a["itok_B_0_15"].reshape(1, NB),
        "wc_in": np.stack([wc, wc.transpose(0, 2, 1)], axis=2),
        "wqkv_in": chunked(a["L0_attn_Wqkv"]),
        "wo_in": chunked(a["L0_attn_Wo"]),
        "w2_in": a["L0_cond2_weight"].transpose(0, 2, 1).reshape(NC, K, P, T).transpose(0, 2, 1, 3).reshape(NC, P, K * T),
        "w_in": chunked(a["L0_ffn_W"].T),
        "ag_in": chunked(np.concatenate([a["L0_ffn_A"], a["L0_ffn_gate_w"]], axis=0).T),
        "bl_in": np.concatenate([bt, bt], axis=0),
        "bias_in": bias,
        "gb_in": a["L0_ffn_gate_b"].reshape(1, G4),
    }
    arrays = {n: np.ascontiguousarray(v) for n, v in arrays.items()}
    nc = bacc.Bacc("TRN2", target_bir_lowering=False, num_devices=1)
    args = {n: nc.dram_tensor(n, v.shape, mybir.dt.from_np(v.dtype), kind="ExternalInput").ap()
            for n, v in arrays.items()}
    out = nc.dram_tensor("out", [NB + NC, P, BT], F32, kind="ExternalOutput").ap()
    x1 = nc.dram_tensor("x1", [NB, P, BT], F32, kind="Internal").ap()
    build(nc, NB, out=out, x1=x1, **args)
    r = run_bass_kernel_spmd(nc, [arrays], core_ids=[0])
    got = np.asarray(r.results[0]["out"])[:NB]
    return np.ascontiguousarray(got.reshape(NB, P, K, S).transpose(0, 3, 2, 1)).reshape(NB, S, T)
```

```python
from contextlib import ExitStack

import concourse.bass as bass
from concourse import mybir

F32, F16, I32 = mybir.dt.float32, mybir.dt.float16, mybir.dt.int32
ALU = mybir.AluOpType
ACT = mybir.ActivationFunctionType
AX = mybir.AxisListType

P = 128
S = 64
T = 1024
K = T // P
DH = 256
NC = 16
R = 64
RANKS = (8, 16, 32, 64)
G4 = len(RANKS)
RG = R + G4
BT = K * S
PT2 = 2 * BT
GR = 2 * PT2
RING = 4
STAGE = 4

SX = 16.0
SZ = 4.0
SC = 16.0
SW = 256.0
SP = 256.0
SU = 32.0
SO = SZ * SU
SQ = SZ * SC

EXP_SCALE = 1.0 / (SQ * SQ * DH ** 0.5)
MASKED = -1.0e30

B_QK, B_V, B_O, B_F, NBIAS = 0, 4, 6, 14, 22


def wait(eng, sem, i, a, b):
    if isinstance(i, int):
        if a * i + b > 0:
            eng.wait_ge(sem, a * i + b)
    else:
        assert a + b > 0, "the first looped step would wait for nothing: peel it"
        eng.wait_ge(sem, a * i + b)


def build(nc, NB, x_in, ids_in, wc_in, wqkv_in, wo_in, w2_in, w_in, ag_in, bl_in, bias_in, gb_in, out, x1):
    NP = NB // 2
    GA = NP // 2
    IA = GA // 2
    NSL, GB, IB = NP, GA, IA
    assert GA % RING == 0 and NB <= P
    FA = 8 * GA

    ctx = ExitStack()
    with ctx:
        def sb(name, shape, dt):
            return ctx.enter_context(nc.sbuf_tensor(name, shape, dt))

        def sem(name):
            return ctx.enter_context(nc.semaphore(name))

        xr = sb("xr", [P, RING * GR], F32)
        stage = sb("stage", [P, STAGE, T], F32)
        w2 = sb("w2", [P, 2, 2 * K * T], F16)
        wf = sb("wf", [P, 2 * K * T], F16)
        wf_h = wf[:, 0:K * T].rearrange("p (k n) -> p k n", k=K)
        wf_l = wf[:, K * T:].rearrange("p (k n) -> p k n", k=K)
        NQ = 3 * DH
        wa = w2[:, 1, :]
        wq_h = wa[:, 0:K * NQ].rearrange("p (k n) -> p k n", k=K)
        wq_l = wa[:, K * NQ:2 * K * NQ].rearrange("p (k n) -> p k n", k=K)
        o0 = 2 * K * NQ
        wo_h = wa[:, o0:o0 + 2 * T].rearrange("p (k n) -> p k n", k=2)
        wo_l = wa[:, o0 + 2 * T:o0 + 4 * T].rearrange("p (k n) -> p k n", k=2)
        ag = sb("ag", [P, K, 2 * RG], F16)
        bl_h = sb("bl_h", [P, T], F16)
        bl_l = sb("bl_l", [P, T], F16)
        xs = sb("xs", [P, 2, K, 2 * P], F16)
        zh_flat = sb("zh", [P, 2 * NQ], F16)
        zl_flat = sb("zl", [P, 2 * NQ], F16)
        zh = zh_flat[:, :].rearrange("p (r n) -> p r n", r=2)
        zl = zl_flat[:, :].rearrange("p (r n) -> p r n", r=2)
        qkh = sb("qkh", [P, 4, P], F16)
        qkl = sb("qkl", [P, 4, P], F16)
        wcf = sb("wcf", [P, 4, 2 * P], F32)
        wch = sb("wch", [P, 2, 2 * P], F16)
        wcl = sb("wcl", [P, 2, 2 * P], F16)
        sm = sb("sm", [P, P], F32)
        ex = sb("ex", [P, P], F32)
        pn = sb("pn", [P, P], F32)
        soft = sb("soft", [P, 4], F32)
        pth = sb("pth", [P, P], F16)
        ptl = sb("ptl", [P, P], F16)
        uh = sb("uh", [P, P], F16)
        ul = sb("ul", [P, P], F16)
        oh = sb("oh", [P, 2, 2, 2 * P], F16)
        ol = sb("ol", [P, 2, 2, 2 * P], F16)
        ft = sb("ft", [P, 2, 2 * P], F32)
        tt = zh_flat[:, 0:8 * P].bitcast(F32).rearrange("p (r m n) -> p r m n", r=2, m=2)
        yf = zl_flat[:, 0:8 * P].bitcast(F32).rearrange("p (r m n) -> p r m n", r=2, m=2)
        yh = sb("yh", [P, 2, K, 2 * P], F16)
        yl_flat = sb("yl", [P, 4 * K * P], F16)
        yl = yl_flat[:, :].rearrange("p (r k n) -> p r k n", r=2, k=K)
        gt = sb("gt", [P, RG], F32)
        gs = sb("gs", [P, 2, RG], F32)
        gb = sb("gb", [P, 2, G4], F32)
        sc = sb("sc", [P, 2, G4], F32)
        pm = sb("pm", [P, 2, 2], F32)
        m012 = sb("m012", [P, 2, 1], F32)
        m123 = sb("m123", [P, 2, 1], F32)
        mx = sb("mx", [P, 2, 1], F32)
        dd = sb("dd", [P, 2, G4], F32)
        ee = sb("ee", [P, 2, G4], F32)
        den = sb("den", [P, 2], F32)
        ptop = sb("ptop", [P, 2], F32)
        itop = sb("itop", [P, 2], F32)
        cw = sb("cw", [P, 2, G4], F32)
        mf = sb("mf", [P, 2, R], F32)
        mhl = sb("mhl", [P, 2, 2 * R], F16)
        mT = sb("mT", [P, 2 * P], F16)
        bias = sb("bias", [P, NBIAS], F32)
        biasq = sb("biasq", [P, 6], F32)
        ident = sb("ident", [P, P], F32)
        ident16 = sb("ident16", [P, P], F16)
        mask = sb("mask", [P, P], F32)
        scratch = yl_flat[:, :].bitcast(F32)
        taken = [0]

        def carve(rows_, n):
            taken[0] += n
            assert taken[0] <= 2 * K * P
            return scratch[0:rows_, taken[0] - n:taken[0]]

        idc_i = sb("idc_i", [P, 1], I32)
        idr_i = sb("idr_i", [P, NB], I32)
        cols = sb("cols", [P, 3], F32)
        idr = carve(P, NB)
        same = carve(P, NB)
        lower = carve(P, NB)
        iota_s = carve(P, NB)
        hot = carve(P, NB)
        used_b = carve(NC, P)
        rank_hot = carve(NC, NC)
        rows = carve(1, 2 * NB + 3 * NC)
        own = sb("own", [P, NC], F32)
        ones = sb("ones", [P, P], F32)
        tri = sb("tri", [NC, 2 * NC], F32)
        iota_e = sb("iota_e", [P, NC], F32)
        place = sb("place", [P, 1], F32)
        per_c = sb("per_c", [NC, 5], F32)
        rank_c = sb("rank_c", [NC, 1], F32)
        ab = sb("ab", [1, 2 * NSL], I32)
        order = sb("order", [1, NB + 2 * NSL + 2 * NC], I32)
        SRC, WAY, NEED, LIST, THRU = 0, NB, NB + NSL, NB + 2 * NSL, NB + 2 * NSL + NC

        bank = [ctx.enter_context(nc.psum_tensor(f"bank{n}", [P, 512], F32)) for n in range(8)]
        zps = [[bank[0], bank[1]], [bank[2], bank[3]]]
        qkps, chps, wops = bank[4], bank[5], [bank[6], bank[7]]
        c2ps, fps, gps, trps = bank[0:4], [bank[4], bank[5]], bank[6], bank[7]
        mtps = trps[:, 0:P].bitcast(F16)

        s_ids, s_small = sem("ids_loaded"), sem("small_loaded")
        s_stage = [sem(f"stage{n}_loaded") for n in range(STAGE)]
        s_pst = [sem(f"pool_stage{n}_loaded") for n in range(STAGE)]
        s_wh, s_wl = sem("weight_hi_made"), sem("weight_lo_made")
        s_pc, s_pw = sem("pool_hi_scaled"), sem("pool_chunk_made")
        s_cst, s_pm0, s_zero = sem("constants_made"), sem("pool_memsets"), sem("zeros_made")
        s_bq = sem("scaled_biases")
        s_sort, s_sp = sem("sort_step"), sem("sort_products")
        s_order = sem("order_ready")
        s_x = [sem("x_even_loaded"), sem("x_odd_loaded")]
        s_st = [sem("x1_even_stored"), sem("x1_odd_stored")]
        s_out = [sem("out_even_stored"), sem("out_odd_stored")]
        s_wc = [sem(f"mix{n}_loaded") for n in range(4)]
        s_xh, s_xl = sem("x_hi"), sem("x_lo")
        s_z, s_zh, s_zl = sem("z_done"), sem("z_hi"), sem("z_lo")
        s_wch, s_wcl = sem("mix_hi"), sem("mix_lo")
        s_qk, s_qkh, s_qkl = sem("qk_done"), sem("qk_hi"), sem("qk_lo")
        s_s, s_sm, s_e, s_r, s_p = sem("scores_done"), sem("scores_masked"), sem("exp_done"), sem("sum_inverted"), sem("probs_ready")
        s_t, s_pth, s_ptl = sem("probs_transposed"), sem("pt_hi"), sem("pt_lo")
        s_u, s_uh, s_ul = sem("u_done"), sem("u_hi"), sem("u_lo")
        s_o, s_oh, s_ol = sem("o_done"), sem("o_hi"), sem("o_lo")
        s_f, s_ft, s_res = sem("out_chunk_done"), sem("out_chunk_biased"), sem("out_chunk_residual")
        s_turn_sp, s_turn_dve, s_turn_pool = sem("sp_turns"), sem("dve_turns"), sem("pool_turns")
        s_c2, s_tt, s_yf, s_yh, s_yl = sem("y_set_done"), sem("y_hilo_copied"), sem("y_summed"), sem("y_hi"), sem("y_lo")
        s_g, s_gt, s_gs = sem("gate_done"), sem("gate_hilo_copied"), sem("gate_summed")
        s_chain, s_dd, s_ee, s_m = sem("gating_step"), sem("gate_shifted"), sem("gate_exp"), sem("middle_ready")
        s_mt, s_mT = sem("middle_transposed"), sem("middle_copied")

        chunks = []
        for k in range(K):
            chunks.append((wqkv_in[:, k * NQ:(k + 1) * NQ], NQ, wq_h[:, k, :], wq_l[:, k, :], None))
        for k in range(2):
            chunks.append((wo_in[:, k * T:(k + 1) * T], T, wo_h[:, k, :], wo_l[:, k, :], None))
        chunks.append((ag_in, K * RG, ag[:, :, 0:RG], ag[:, :, RG:2 * RG], K))
        chunks.append((bl_in, T, bl_h[:, :], bl_l[:, :], None))
        NCH = len(chunks)
        assert NCH % STAGE == 0 and K % STAGE == 0

        def group_cols(g, lo=0, n=GR):
            return xr[:, bass.ds((g % RING) * GR + lo, n)]

        def batch_view(i, q, b):
            v = group_cols(2 * i + q // 2, (q % 2) * PT2 + b * BT, BT)
            return v.rearrange("p (k s) -> p k s", k=K)

        def split_view(q, b, half):
            return xs[:, q % 2, :, half * P + b * S:half * P + (b + 1) * S]

        def chunk_view(g, m):
            return group_cols(g).rearrange("p (b k s) -> p b k s", b=4, k=K)[:, :, m, :]

        def group_before(i, u):
            if u == 1:
                return i, 0
            return None if isinstance(i, int) and i == 0 else (i - 1, 1)

        def x_ready(eng, i, q, phase_b):
            u = (q // 2) % 2
            n = q // 4
            if phase_b:
                wait(eng, s_x[u], i, 64, 16 * IA + 64 * (n + 1))
            else:
                wait(eng, s_x[u], i, 16, 16 * (n + 1))

        block = ctx.enter_context(nc.Block())

        @block.sync
        def _(sp):
            def load_x(i, u):
                sp.dma_start(group_cols(2 * i + u), x_in[bass.ds(2 * i + u, 1), :, :].rearrange("a p n -> (a p) n")
                             ).then_inc(s_x[u], 16)

            def load_mix(i, q):
                n = q % 4
                wait(sp, s_wcl, i, 4, q - 3)
                sp.sem_inc(s_turn_sp, 1)
                for b in range(2):
                    e = sp.value_load(idr_i[0:1, bass.ds(8 * i + 2 * q + b, 1)], min_val=0, max_val=NC - 1)
                    dst = wcf[b * S:(b + 1) * S, n, :].rearrange("p (t d) -> p t d", t=2)[:, :, b * S:(b + 1) * S]
                    src = wc_in[bass.ds(e, 1), :, :, :].rearrange("a c t d -> (a c) t d")
                    sp.dma_start(dst, src).then_inc(s_wc[n], 16)

            def load_chunk(n):
                src, w = chunks[n][0], chunks[n][1]
                if n >= STAGE:
                    sp.wait_ge(s_wl, n - STAGE + 1)
                sp.dma_start(stage[:, n % STAGE, 0:w], src).then_inc(s_stage[n % STAGE], 16)

            def store_x1(i, u):
                wait(sp, s_res, i, 16, 8 * (u + 1))
                sp.sem_inc(s_turn_sp, 1)
                sp.dma_start(x1[bass.ds(4 * (2 * i + u), 4), :, :].rearrange("b p n -> p b n"),
                             group_cols(2 * i + u).rearrange("p (b n) -> p b n", b=4)).then_inc(s_st[u], 16)

            sp.dma_start(idr_i[:, :], ids_in.to_broadcast([P, NB])).then_inc(s_ids, 16)
            sp.dma_start(idc_i[0:NB, :], ids_in.rearrange("a b -> b a")).then_inc(s_ids, 16)
            load_x(0, 0)
            load_chunk(0)
            load_chunk(1)
            sp.dma_start(bias[:, :], bias_in).then_inc(s_small, 16)
            for h in range(2):
                sp.dma_start(gb[:, h, :], gb_in.to_broadcast([P, G4])).then_inc(s_small, 16)
            load_chunk(2)
            load_chunk(3)
            sp.wait_ge(s_ids, 32)
            sp.wait_ge(s_zero, 1)
            load_mix(0, 0)
            load_mix(0, 1)
            for n in range(STAGE, NCH):
                load_chunk(n)
                if n == STAGE:
                    load_x(0, 1)

            def body(i, first=False, last=False):
                for u in range(2):
                    if not last:
                        wait(sp, s_st[u], i, 16, 0)
                        sp.sem_inc(s_turn_sp, 1)
                        wait(sp, s_x[u], i, 16, 16)
                        sp.sem_inc(s_turn_sp, 1)
                        load_x(i + 1, u)
                    for j in range(2):
                        q = 2 * u + j
                        if not (last and q >= 2):
                            load_mix(i, q + 2)
                    if u == 1:
                        store_x1(i, 0)
                    elif not first:
                        store_x1(i - 1, 1)

            body(0, first=True)
            with sp.Fori(1, IA - 1) as i:
                body(i)
            body(IA - 1, last=True)
            store_x1(IA - 1, 1)

            def load_slots(i, u):
                for b in range(4):
                    r = sp.value_load(order[0:1, bass.ds(SRC + 4 * (2 * i + u) + b, 1)], min_val=0, max_val=NB - 1)
                    sp.dma_start(group_cols(2 * i + u, b * BT, BT),
                                 x1[bass.ds(r, 1), :, :].rearrange("a p n -> (a p) n")).then_inc(s_x[u], 16)

            def store_out(i, u):
                wait(sp, s_res, i, 16, FA + 8 * (u + 1))
                sp.sem_inc(s_turn_sp, 1)
                for b in range(4):
                    r = sp.value_load(order[0:1, bass.ds(SRC + 4 * (2 * i + u) + b, 1)], min_val=0, max_val=NB - 1)
                    sp.dma_start(out[bass.ds(r, 1), :, :].rearrange("a p n -> (a p) n"),
                                 group_cols(2 * i + u, b * BT, BT)).then_inc(s_out[u], 16)

            for u in range(2):
                sp.wait_ge(s_st[u], 16 * IA)
            sp.wait_ge(s_order, 1)
            for u in range(2):
                load_slots(0, u)

            def body_b(i, first=False, last=False):
                for u in range(2):
                    if not last:
                        wait(sp, s_out[u], i, 64, 0)
                        sp.sem_inc(s_turn_sp, 1)
                        wait(sp, s_x[u], i, 64, 16 * IA + 64)
                        sp.sem_inc(s_turn_sp, 1)
                        load_slots(i + 1, u)
                    if u == 1:
                        store_out(i, 0)
                    elif not first:
                        store_out(i - 1, 1)

            body_b(0, first=True)
            with sp.Fori(1, IB - 1) as i:
                body_b(i)
            body_b(IB - 1, last=True)
            store_out(IB - 1, 1)
            for u in range(2):
                sp.wait_ge(s_out[u], 64 * IB)

        @block.gpsimd
        def _(pool):
            pool.memset(ident[:, :], 0.0).then_inc(s_pm0, 1)
            pool.memset(ones[:, :], 1.0).then_inc(s_pm0, 1)
            pool.memset(per_c[:, 2:3], 1.0).then_inc(s_pm0, 1)
            pool.iota(cols[:, 0:1], pattern=[[0, 1]], base=0, channel_multiplier=1,
                      allow_small_or_imprecise_dtypes=True).then_inc(s_cst, 1)
            pool.iota(iota_e[:, :], pattern=[[1, NC]], base=0, channel_multiplier=0,
                      allow_small_or_imprecise_dtypes=True).then_inc(s_cst, 1)
            pool.iota(iota_s[:, :], pattern=[[1, NB]], base=0, channel_multiplier=0,
                      allow_small_or_imprecise_dtypes=True).then_inc(s_cst, 1)
            pool.iota(per_c[:, 0:1], pattern=[[0, 1]], base=0, channel_multiplier=1,
                      allow_small_or_imprecise_dtypes=True).then_inc(s_cst, 1)
            pool.wait_ge(s_pm0, 3)
            pool.affine_select(out=lower[:, :], in_=ones[:, 0:NB], compare_op=ALU.is_gt, fill=0.0, base=0,
                               pattern=[[-1, NB]], channel_multiplier=1).then_inc(s_cst, 1)
            pool.wait_ge(s_cst, 5)
            pool.affine_select(out=tri[:, 0:NC], in_=ones[0:NC, 0:NC], compare_op=ALU.is_gt, fill=0.0, base=0,
                               pattern=[[1, NC]], channel_multiplier=-1).then_inc(s_cst, 1)
            pool.wait_ge(s_cst, 6)
            pool.affine_select(out=tri[:, NC:2 * NC], in_=ones[0:NC, 0:NC], compare_op=ALU.is_ge, fill=0.0, base=0,
                               pattern=[[1, NC]], channel_multiplier=-1).then_inc(s_cst, 1)
            pool.wait_ge(s_cst, 7)
            pool.affine_select(out=ident[:, :], in_=ident[:, :], compare_op=ALU.not_equal, fill=1.0, base=0,
                               pattern=[[-1, P]], channel_multiplier=1).then_inc(s_cst, 1)
            pool.wait_ge(s_cst, 8)
            pool.tensor_copy(ident16[:, :], ident[:, :]).then_inc(s_cst, 1)

            def load(src, st):
                pool.dma_start(stage[:, st, :], src).then_inc(s_pst[st], 16)

            def split(hi, lo, t, reload):
                def low(k):
                    pool.wait_ge(s_pc, 2 * K * t + 2 * k + 2)
                    pool.tensor_tensor(lo[:, k, :], stage[:, k % STAGE, :], hi[:, k, :], ALU.subtract
                                       ).then_inc(s_pw, 1)

                for k in range(K):
                    st = stage[:, k % STAGE, :]
                    pool.wait_ge(s_pst[k % STAGE], 16 * (K // STAGE) * t + 16 * (k // STAGE + 1))
                    pool.sem_inc(s_turn_pool, 1)
                    pool.tensor_scalar(hi[:, k, :], st, SW, 1.0, ALU.mult, ALU.mult).then_inc(s_pc, 1)
                    pool.tensor_scalar(st, st, SW, 1.0, ALU.mult, ALU.mult).then_inc(s_pc, 1)
                    if k > 0:
                        low(k - 1)
                    if k > 1:
                        pool.wait_ge(s_pw, K * t + k - 1)
                        reload(k - 2)
                low(K - 1)
                for k in (K - 2, K - 1):
                    pool.wait_ge(s_pw, K * t + k + 1)
                    reload(k)

            def reloader(here, after):
                def reload(k):
                    if k < K - STAGE:
                        here(k + STAGE)
                    else:
                        after(k + STAGE - K)
                return reload

            def load_w(k):
                load(w_in[:, k * T:(k + 1) * T], k % STAGE)

            def load_w2(r):
                def chunk(k):
                    pool.sem_inc(s_turn_pool, 1)
                    e = pool.value_load(order[0:1, bass.ds(LIST + r, 1)], min_val=0, max_val=NC - 1)
                    load(w2_in[bass.ds(e, 1), :, k * T:(k + 1) * T].rearrange("a p n -> (a p) n"), k % STAGE)
                return chunk

            pool.wait_ge(s_wl, NCH)
            pool.wait_ge(s_order, 1)
            for k in range(STAGE):
                load_w(k)
            split(wf_h, wf_l, 0, reloader(load_w, load_w2(0)))

            def condition(i, b, more=True):
                r = 2 * i + b
                hi = w2[:, b, 0:K * T].rearrange("p (k n) -> p k n", k=K)
                lo = w2[:, b, K * T:].rearrange("p (k n) -> p k n", k=K)
                split(hi, lo, r + 1, reloader(load_w2(r), load_w2(r + 1) if more else lambda k: None))

            def free_buffer(i, b):
                n = pool.value_load(order[0:1, bass.ds(THRU + 2 * i + b - 2, 1)], min_val=0, max_val=NSL)
                pool.wait_ge(s_c2, 4 * n + 1)
                pool.sem_inc(s_turn_pool, 1)

            condition(0, 0)
            pool.wait_ge(s_f, FA)
            condition(0, 1)
            with pool.Fori(1, NC // 2 - 1) as i:
                for b in range(2):
                    free_buffer(i, b)
                    condition(i, b)
            i = NC // 2 - 1
            free_buffer(i, 0)
            condition(i, 0)
            free_buffer(i, 1)
            condition(i, 1, more=False)

        @block.scalar
        def _(act):
            Copy, Iden = ACT.Copy, ACT.Identity

            act.wait_ge(s_small, 48)
            nc.scalar.activation(biasq[:, 0:4], bias[:, B_QK:B_QK + 4], Copy, scale=SQ).then_inc(s_bq, 1)
            nc.scalar.activation(biasq[:, 4:6], bias[:, B_V:B_V + 2], Copy, scale=SO).then_inc(s_bq, 1)

            def x_hi(i, q, phase_b=False):
                x_ready(act, i, q, phase_b)
                for b in range(2):
                    last = nc.scalar.activation(split_view(q, b, 0), batch_view(i, q, b), Copy, scale=SX)
                last.then_inc(s_xh, 1)

            def mix_hi(i, q):
                wait(act, s_wc[q % 4], i, 32, 32 * (q // 4 + 1))
                wait(act, s_u, i, 4, q - 1)
                nc.scalar.activation(wch[:, q % 2, :], wcf[:, q % 4, :], Copy, scale=SC).then_inc(s_wch, 1)

            x_hi(0, 0)
            def chunk_hi(n):
                _, w, hi, _, k = chunks[n]
                act.wait_ge(s_stage[n % STAGE], 16 * (n // STAGE + 1))
                src = stage[:, n % STAGE, 0:w]
                if k:
                    src = src.rearrange("p (k n) -> p k n", k=k)
                nc.scalar.activation(hi, src, Copy, scale=SW).then_inc(s_wh, 1)

            for n in range(K):
                chunk_hi(n)
            mix_hi(0, 0)
            x_hi(0, 1)

            def out_chunks(i, u, ms, n0, scale, b0):
                for m in ms:
                    wait(act, s_f, i, 16, n0 + 8 * u + m + 1)
                    wait(act, s_res, i, 16, n0 + 8 * u + m - 1)
                    src = (wops if n0 == 0 else fps)[m % 2]
                    nc.scalar.activation(ft[:, m % 2, :], src[:, 0:2 * P], Iden, bias=bias[:, b0 + m:b0 + m + 1],
                                         scale=scale).then_inc(s_ft, 1)

            def z_hi(i, q):
                wait(act, s_z, i, 4, q + 1)
                for h in range(2):
                    e = nc.scalar.activation(zh[:, q % 2, h * 384:(h + 1) * 384], zps[q % 2][h][:, 0:384], Copy,
                                             scale=SZ / (SX * SW))
                e.then_inc(s_zh, 1)

            def a_step(i, q, last=False):
                u, j = q // 2, q % 2
                before = group_before(i, u)

                def oo(n):
                    if before:
                        out_chunks(*before, [4 * j + n], 0, 1.0 / (SO * SW), B_O)

                wait(act, s_qk, i, 4, q + 1)
                for c in range(4):
                    e = nc.scalar.activation(qkh[:, c, :], qkps[:, c * P:(c + 1) * P], Iden, bias=biasq[:, c:c + 1])
                e.then_inc(s_qkh, 1)
                if not (last and q == 3):
                    mix_hi(i, q + 1)
                oo(0)
                wait(act, s_sm, i, 4, q + 1)
                nc.scalar.activation(ex[:, :], sm[:, :], ACT.Exp, bias=soft[:, 0:1], scale=-1.0,
                                     accum_out=soft[:, 1:2]).then_inc(s_e, 1)
                if not (last and q >= 2):
                    x_hi(i, q + 2)
                oo(1)
                wait(act, s_t, i, 4, q + 1)
                nc.scalar.copy(pth[:, :], chps[:, 0:P]).then_inc(s_pth, 1)
                oo(2)
                wait(act, s_u, i, 4, q + 1)
                nc.scalar.activation(uh[:, :], chps[:, 0:P], Copy, scale=SU / (SC * SP)).then_inc(s_uh, 1)
                if not (last and q == 3):
                    z_hi(i, q + 1)
                oo(3)
                wait(act, s_o, i, 4, q + 1)
                for c in range(2):
                    e = nc.scalar.activation(oh[:, u, c, j * P:(j + 1) * P], chps[:, c * P:(c + 1) * P], Iden,
                                             bias=biasq[:, 4 + c:5 + c])
                e.then_inc(s_oh, 1)

            def a_body(i, last=False):
                for q in range(4):
                    a_step(i, q, last)

            act.wait_ge(s_bq, 2)
            z_hi(0, 0)
            for q in range(4):
                a_step(0, q)
                if q < 2:
                    chunk_hi(K + 2 * q)
                    chunk_hi(K + 2 * q + 1)
            with act.Fori(1, IA - 1) as i:
                a_body(i)
            a_body(IA - 1, last=True)
            out_chunks(IA - 1, 1, range(K), 0, 1.0 / (SO * SW), B_O)

            def y_set(i, q, t):
                wait(act, s_c2, i, 16, 4 * q + t + 2)
                wait(act, s_yf, i, 16, 4 * q + t - 1)
                src = c2ps[t][:, :].rearrange("p (m h n) -> p m h n", m=2, h=2)
                nc.scalar.activation(tt[:, t % 2, :, :], src[:, :, 1, :], Copy, scale=1.0 / SW).then_inc(s_tt, 1)
                wait(act, s_yf, i, 16, 4 * q + t + 1)
                nc.scalar.copy(yh[:, q // 2, 2 * t:2 * t + 2, (q % 2) * P:(q % 2 + 1) * P], yf[:, t % 2, :, :]).then_inc(s_yh, 1)

            def gate_copy(i, q):
                wait(act, s_g, i, 4, q + 1)
                wait(act, s_gs, i, 4, q)
                nc.scalar.copy(gt[:, :], gps[:, RG:2 * RG]).then_inc(s_gt, 1)

            def gate_exp(i, u):
                wait(act, s_dd, i, 2, u + 1)
                nc.scalar.activation(ee[:, :, :], dd[:, :, :], ACT.Exp).then_inc(s_ee, 1)

            def middle_copy(i, u):
                wait(act, s_mt, i, 2, u + 1)
                nc.scalar.copy(mT[:, :], mtps).then_inc(s_mT, 1)

            def b_step(i, q, first=False, last=False):
                u, j = q // 2, q % 2
                pi, pu = (i, 0) if u == 1 else (i - 1, 1)
                y_set(i, q, 0)
                if q > 0:
                    gate_copy(i, q - 1)
                elif not first:
                    gate_copy(i - 1, 3)
                before = not (first and u == 0)
                if j == 0 and before:
                    gate_exp(pi, pu)
                y_set(i, q, 1)
                if not (last and q == 3):
                    x_hi(i, q + 1, phase_b=True)
                y_set(i, q, 2)
                y_set(i, q, 3)
                if j == 0 and before:
                    middle_copy(pi, pu)
                if before:
                    out_chunks(pi, pu, range(4 * j, 4 * j + 4), FA, 1.0 / (SX * SW), B_F)

            def b_body(i, first=False, last=False):
                for q in range(4):
                    b_step(i, q, first, last)

            x_hi(0, 0, phase_b=True)
            b_body(0, first=True)
            with act.Fori(1, IB - 1) as i:
                b_body(i)
            b_body(IB - 1, last=True)
            gate_copy(IB - 1, 3)
            gate_exp(IB - 1, 1)
            middle_copy(IB - 1, 1)
            out_chunks(IB - 1, 1, range(K), FA, 1.0 / (SX * SW), B_F)

        @block.vector
        def _(dve):
            v = nc.vector
            v.memset(wcf[:, :, :], 0.0).then_inc(s_zero, 1)
            for a in range(2):
                for b in range(2):
                    v.memset(mask[a * S:(a + 1) * S, b * S:(b + 1) * S], 0.0 if a == b else MASKED).then_inc(s_zero, 1)

            done = [0]

            def link(ins):
                done[0] += 1
                ins.then_inc(s_sort, 1)
                dve.wait_ge(s_sort, done[0])


            def find_places():
                dve.wait_ge(s_ids, 32)
                dve.wait_ge(s_cst, 9)
                dve.wait_ge(s_zero, 5)
                link(v.tensor_copy(cols[0:NB, 2:3], idc_i[0:NB, :]))
                link(v.tensor_copy(idr[0:NB, :], idr_i[0:NB, :]))
                link(v.tensor_scalar(own[0:NB, :], iota_e[0:NB, :], cols[0:NB, 2:3], None, ALU.is_equal))
                link(v.tensor_scalar(same[0:NB, :], idr[0:NB, :], cols[0:NB, 2:3], None, ALU.is_equal))
                link(v.tensor_tensor(same[0:NB, :], same[0:NB, :], lower[0:NB, :], ALU.mult))
                link(v.tensor_scalar(idr[0:NB, :], idr[0:NB, :], cols[0:NB, 2:3], None, ALU.is_lt))
                link(v.tensor_tensor_reduce(out=idr[0:NB, :], in0=idr[0:NB, :], in1=same[0:NB, :], scale=1.0, scalar=0.0,
                                            op0=ALU.add, op1=ALU.add, accum_out=place[0:NB, :]))
                link(v.tensor_scalar(hot[0:NB, :], iota_s[0:NB, :], place[0:NB, :], None, ALU.is_equal))

            def rank_conditions():
                dve.wait_ge(s_sp, 1)
                link(v.tensor_copy(per_c[:, 3:4], trps[0:NC, 0:1]))
                link(v.tensor_scalar(per_c[:, 4:5], per_c[:, 3:4], 1.0, None, ALU.min))
                link(v.tensor_scalar(used_b[:, :], ones[0:NC, :], per_c[:, 4:5], None, ALU.mult))
                dve.wait_ge(s_sp, 2)
                link(v.tensor_tensor_reduce(out=own[0:NB, :], in0=own[0:NB, :], in1=trps[0:NB, 0:NC], scale=1.0,
                                            scalar=0.0, op0=ALU.mult, op1=ALU.add, accum_out=cols[0:NB, 1:2]))
                link(v.tensor_copy(rank_c[:, :], trps[0:NC, NC:NC + 1]))
                link(v.tensor_copy(per_c[:, 1:2], trps[0:NC, NC + 1:NC + 2]))
                link(v.tensor_scalar(rank_hot[:, :], iota_e[0:NC, :], rank_c[:, :], per_c[:, 4:5], ALU.is_equal, ALU.mult))

            def write_order():
                dve.wait_ge(s_sp, 3)
                link(v.tensor_copy(rows[:, :], trps[0:1, 0:2 * NB + 3 * NC]))
                link(v.tensor_copy(order[0:1, SRC:SRC + NB], rows[:, 0:NB]))
                link(v.tensor_copy(order[0:1, LIST:LIST + NC], rows[:, 2 * NB:2 * NB + NC]))
                upto = rows[:, 2 * NB + NC:2 * NB + 2 * NC]
                occurs = rows[:, 2 * NB + 2 * NC:2 * NB + 3 * NC]
                link(v.scalar_tensor_tensor(out=upto, in0=occurs, scalar=-float(NB), in1=upto, op0=ALU.mult, op1=ALU.add))
                link(v.tensor_scalar(order[0:1, THRU:THRU + NC], upto, float(NB + 1), None, ALU.add))
                link(v.tensor_scalar(order[0:1, THRU:THRU + NC], order[0:1, THRU:THRU + NC], 1, None,
                                     ALU.logical_shift_right))
                two = rows[:, NB:2 * NB].rearrange("p (s h) -> p s h", h=2)
                first, second = ab[:, 0:NSL], ab[:, NSL:2 * NSL]
                link(v.tensor_copy(first, two[:, :, 0]))
                link(v.tensor_copy(order[0:1, NEED:NEED + NSL], two[:, :, 1]))
                link(v.tensor_scalar(first, first, 1, None, ALU.bitwise_and))
                link(v.tensor_tensor(second, two[:, :, 1], two[:, :, 0], ALU.subtract))
                link(v.tensor_scalar(second, second, 1, None, ALU.logical_shift_left))
                v.tensor_tensor(order[0:1, WAY:WAY + NSL], first, second, ALU.bitwise_or).then_inc(s_order, 1)

            def x_lo(i, q, b, phase_b=False):
                x_ready(dve, i, q, phase_b)
                wait(dve, s_xh, i, 4, (NP if phase_b else 0) + q + 1)
                e = v.scalar_tensor_tensor(out=split_view(q, b, 1), in0=batch_view(i, q, b), scalar=SX,
                                           in1=split_view(q, b, 0), op0=ALU.mult, op1=ALU.subtract)
                if b == 1:
                    e.then_inc(s_xl, 1)

            def mix_lo(i, q):
                wait(dve, s_wch, i, 4, q + 1)
                v.scalar_tensor_tensor(out=wcl[:, q % 2, :], in0=wcf[:, q % 4, :], scalar=SC, in1=wch[:, q % 2, :],
                                       op0=ALU.mult, op1=ALU.subtract).then_inc(s_wcl, 1)

            for b in range(2):
                x_lo(0, 0, b)
            def chunk_lo(n):
                _, w, hi, lo, k = chunks[n]
                dve.wait_ge(s_wh, n + 1)
                src = stage[:, n % STAGE, 0:w]
                if k:
                    src = src.rearrange("p (k n) -> p k n", k=k)
                v.scalar_tensor_tensor(out=lo, in0=src, scalar=SW, in1=hi, op0=ALU.mult,
                                       op1=ALU.subtract).then_inc(s_wl, 1)

            for n in range(K):
                chunk_lo(n)
            mix_lo(0, 0)
            for b in range(2):
                x_lo(0, 1, b)

            def residual(i, u, ms, n0):
                for m in ms:
                    wait(dve, s_ft, i, 16, n0 + 8 * u + m + 1)
                    ring = chunk_view(2 * i + u, m)
                    v.tensor_tensor(ring, ft[:, m % 2, :].rearrange("p (b s) -> p b s", b=4), ring,
                                    ALU.add).then_inc(s_res, 1)

            def z_lo(i, q):
                wait(dve, s_zh, i, 4, q + 1)
                for h in range(2):
                    c = slice(h * 384, (h + 1) * 384)
                    e = v.scalar_tensor_tensor(out=zl[:, q % 2, c], in0=zps[q % 2][h][:, 0:384],
                                               scalar=SZ / (SX * SW), in1=zh[:, q % 2, c], op0=ALU.mult,
                                               op1=ALU.subtract)
                e.then_inc(s_zl, 1)

            def a_step(i, q, last=False):
                u, j = q // 2, q % 2
                before = group_before(i, u)

                def oo(n):
                    if before:
                        residual(*before, [4 * j + n], 0)

                wait(dve, s_qkh, i, 4, q + 1)
                for c in range(4):
                    e = v.scalar_tensor_tensor(out=qkl[:, c, :], in0=qkps[:, c * P:(c + 1) * P],
                                               scalar=biasq[:, c:c + 1], in1=qkh[:, c, :], op0=ALU.add,
                                               op1=ALU.subtract)
                e.then_inc(s_qkl, 1)
                if not (last and q == 3):
                    mix_lo(i, q + 1)
                oo(0)
                wait(dve, s_s, i, 4, q + 1)
                dve.sem_inc(s_turn_dve, 1)
                v.tensor_tensor_reduce(out=sm[:, :], in0=chps[:, 0:P], in1=mask[:, :], scale=-EXP_SCALE,
                                       scalar=3.0e38, op0=ALU.add, op1=ALU.min,
                                       accum_out=soft[:, 0:1]).then_inc(s_sm, 1)
                wait(dve, s_e, i, 4, q + 1)
                v.reciprocal(soft[:, 2:3], soft[:, 1:2]).then_inc(s_r, 1)
                wait(dve, s_r, i, 4, q + 1)
                v.tensor_scalar(pn[:, :], ex[:, :], soft[:, 2:3], SP, ALU.mult, ALU.mult).then_inc(s_p, 1)
                if not (last and q >= 2):
                    x_lo(i, q + 2, 0)
                oo(1)
                wait(dve, s_pth, i, 4, q + 1)
                v.tensor_tensor(ptl[:, :], chps[:, 0:P], pth[:, :], ALU.subtract).then_inc(s_ptl, 1)
                if not (last and q >= 2):
                    x_lo(i, q + 2, 1)
                oo(2)
                wait(dve, s_uh, i, 4, q + 1)
                v.scalar_tensor_tensor(out=ul[:, :], in0=chps[:, 0:P], scalar=SU / (SC * SP), in1=uh[:, :],
                                       op0=ALU.mult, op1=ALU.subtract).then_inc(s_ul, 1)
                if not (last and q == 3):
                    z_lo(i, q + 1)
                oo(3)
                wait(dve, s_oh, i, 4, q + 1)
                for c in range(2):
                    e = v.scalar_tensor_tensor(out=ol[:, u, c, j * P:(j + 1) * P], in0=chps[:, c * P:(c + 1) * P],
                                               scalar=biasq[:, 4 + c:5 + c], in1=oh[:, u, c, j * P:(j + 1) * P],
                                               op0=ALU.add, op1=ALU.subtract)
                e.then_inc(s_ol, 1)

            def a_body(i, last=False):
                for q in range(4):
                    a_step(i, q, last)

            z_lo(0, 0)
            find_places()
            for q in range(4):
                a_step(0, q)
                if q == 0:
                    rank_conditions()
                if q == 1:
                    write_order()
                if q < 2:
                    chunk_lo(K + 2 * q)
                    chunk_lo(K + 2 * q + 1)
            with dve.Fori(1, IA - 1) as i:
                a_body(i)
            a_body(IA - 1, last=True)
            residual(IA - 1, 1, range(K), 0)

            def y_set(i, q, t):
                wait(dve, s_yl, i, 16, 4 * q + t - 1)
                wait(dve, s_tt, i, 16, 4 * q + t + 1)
                src = c2ps[t][:, :].rearrange("p (m h n) -> p m h n", m=2, h=2)
                v.scalar_tensor_tensor(out=yf[:, t % 2, :, :], in0=src[:, :, 0, :], scalar=1.0 / SW, in1=tt[:, t % 2, :, :],
                                       op0=ALU.mult, op1=ALU.add).then_inc(s_yf, 1)
                wait(dve, s_yh, i, 16, 4 * q + t + 1)
                c = slice((q % 2) * P, (q % 2 + 1) * P)
                v.tensor_tensor(yl[:, q // 2, 2 * t:2 * t + 2, c], yf[:, t % 2, :, :], yh[:, q // 2, 2 * t:2 * t + 2, c],
                                ALU.subtract).then_inc(s_yl, 1)

            def gate_sum(i, q):
                wait(dve, s_gt, i, 4, q + 1)
                v.tensor_tensor(gs[:, q % 2, :], gps[:, 0:RG], gt[:, :], ALU.add).then_inc(s_gs, 1)

            STEPS = 12

            def gating(i, u, part):
                n = [0 if part == 1 else 5]

                def link(ins):
                    n[0] += 1
                    ins.then_inc(s_chain, 1)
                    wait(dve, s_chain, i, 2 * STEPS, u * STEPS + n[0])

                if part == 1:
                    wait(dve, s_gs, i, 4, 2 * u + 2)
                    link(v.scalar_tensor_tensor(out=sc[:, :, :], in0=gs[:, :, R:RG], scalar=1.0 / (SX * SW),
                                                in1=gb[:, :, :], op0=ALU.mult, op1=ALU.add))
                    pairs = sc[:, :, :].rearrange("p h (a b) -> p h a b", b=2)
                    link(v.tensor_tensor(pm[:, :, :], pairs[:, :, :, 0], pairs[:, :, :, 1], ALU.max))
                    link(v.tensor_tensor(m012[:, :, :], pm[:, :, 0:1], sc[:, :, 2:3], ALU.max))
                    link(v.tensor_tensor(m123[:, :, :], pm[:, :, 1:2], sc[:, :, 1:2], ALU.max))
                    link(v.tensor_tensor(mx[:, :, :], pm[:, :, 0:1], pm[:, :, 1:2], ALU.max))
                    v.tensor_tensor(dd[:, :, :], sc[:, :, :], mx[:, :, :].to_broadcast([P, 2, G4]),
                                    ALU.subtract).then_inc(s_dd, 1)
                    return
                wait(dve, s_ee, i, 2, u + 1)
                link(v.reduce_sum(den[:, :], ee[:, :, :], axis=AX.X))
                link(v.reciprocal(ptop[:, :], den[:, :]))
                link(v.reciprocal(itop[:, :], ptop[:, :]))
                w = cw[:, :, 0:1]
                link(v.tensor_tensor(w, ptop[:, :].rearrange("p (h a) -> p h a", a=1),
                                     itop[:, :].rearrange("p (h a) -> p h a", a=1), ALU.mult))
                v.tensor_tensor(cw[:, :, 1:2], m123[:, :, :], sc[:, :, 0:1], ALU.is_gt)
                v.tensor_tensor(cw[:, :, 2:3], pm[:, :, 1:2], pm[:, :, 0:1], ALU.is_gt)
                link(v.tensor_tensor(cw[:, :, 3:4], sc[:, :, 3:4], m012[:, :, :], ALU.is_gt))
                lo = 0
                for r, hi in enumerate(RANKS):
                    n_c = hi - lo
                    f = cw[:, :, r:r + 1].to_broadcast([P, 2, n_c])
                    e = v.scalar_tensor_tensor(out=mf[:, :, lo:hi], in0=gs[:, :, lo:hi], scalar=1.0 / SW, in1=f,
                                               op0=ALU.mult, op1=ALU.mult)
                    lo = hi
                link(e)
                v.tensor_tensor(mf[:, :, RANKS[0]:R], mf[:, :, RANKS[0]:R],
                                w.to_broadcast([P, 2, R - RANKS[0]]), ALU.mult).then_inc(s_chain, 1)
                wait(dve, s_chain, i, 2 * STEPS, (u + 1) * STEPS)
                v.tensor_copy(mhl[:, :, 0:R], mf[:, :, :]).then_inc(s_m, 1)
                wait(dve, s_m, i, 4, 2 * u + 1)
                v.tensor_tensor(mhl[:, :, R:2 * R], mf[:, :, :], mhl[:, :, 0:R], ALU.subtract).then_inc(s_m, 1)

            def b_step(i, q, first=False, last=False):
                u, j = q // 2, q % 2
                pi, pu = (i, 0) if u == 1 else (i - 1, 1)
                before = not (first and u == 0)
                y_set(i, q, 0)
                if q > 0:
                    gate_sum(i, q - 1)
                elif not first:
                    gate_sum(i - 1, 3)
                if j == 0 and before:
                    gating(pi, pu, 1)
                y_set(i, q, 1)
                if j == 0 and before:
                    gating(pi, pu, 2)
                if not (last and q == 3):
                    for b in range(2):
                        x_lo(i, q + 1, b, phase_b=True)
                y_set(i, q, 2)
                y_set(i, q, 3)
                if before:
                    residual(pi, pu, range(4 * j, 4 * j + 4), FA)

            def b_body(i, first=False, last=False):
                for q in range(4):
                    b_step(i, q, first, last)

            for b in range(2):
                x_lo(0, 0, b, phase_b=True)
            b_body(0, first=True)
            with dve.Fori(1, IB - 1) as i:
                b_body(i)
            b_body(IB - 1, last=True)
            gate_sum(IB - 1, 3)
            gating(IB - 1, 1, 1)
            gating(IB - 1, 1, 2)
            residual(IB - 1, 1, range(K), FA)

        @block.tensor
        def _(pe):
            mm = nc.tensor.matmul

            def three(dst, pairs, first=True, last=True):
                n = len(pairs)
                for k, (ah, al, bh, bl) in enumerate(pairs):
                    mm(dst, ah, bh, start=first and k == 0, stop=False)
                    mm(dst, ah, bl, start=False, stop=False)
                    e = mm(dst, al, bh, start=False, stop=last and k == n - 1)
                return e

            def sort_counts():
                pe.wait_ge(s_cst, 9)
                pe.wait_ge(s_sort, 3)
                mm(trps[0:NC, 0:1], own[0:NB, :], ones[0:NB, 0:1], start=True, stop=True).then_inc(s_sp, 1)

            def sort_ranks():
                pe.wait_ge(s_sort, 11)
                mm(trps[:, 0:NC], used_b[:, :], tri[:, 0:NC], start=True, stop=True)
                mm(trps[0:NC, NC:NC + 1], tri[:, 0:NC], per_c[:, 4:5], start=True, stop=True)
                mm(trps[0:NC, NC + 1:NC + 2], tri[:, NC:2 * NC], per_c[:, 3:4], start=True, stop=True
                   ).then_inc(s_sp, 1)

            def sort_rows():
                pe.wait_ge(s_sort, 15)
                for r in range(2):
                    mm(trps[0:1, r * NB:(r + 1) * NB], cols[0:NB, r:r + 1], hot[0:NB, :], start=True, stop=True)
                for r in range(3):
                    e = mm(trps[0:1, 2 * NB + r * NC:2 * NB + (r + 1) * NC], per_c[:, r:r + 1], rank_hot[:, :],
                           start=True, stop=True)
                e.then_inc(s_sp, 1)

            def z_part(i, q, ks, start_up=False):
                if ks[0] == 0:
                    wait(pe, s_xl, i, 4, q + 1)
                    wait(pe, s_zl, i, 4, q - 1)
                for k in ks:
                    if start_up:
                        pe.wait_ge(s_wl, k + 1)
                    a, b = xs[:, q % 2, k, 0:P], xs[:, q % 2, k, P:2 * P]
                    for lhs, rhs in ((a, wq_h), (a, wq_l), (b, wq_h)):
                        for h in range(2):
                            e = mm(zps[q % 2][h][:, 0:384], lhs, rhs[:, k, h * 384:(h + 1) * 384],
                                   start=(k == 0 and lhs is a and rhs is wq_h),
                                   stop=(k == K - 1 and lhs is b))
                if ks[-1] == K - 1:
                    e.then_inc(s_z, 1)

            def out_products(i, u, ms):
                wait(pe, s_ol, i, 4, 2 * u + 2)
                for m in ms:
                    wait(pe, s_ft, i, 16, 8 * u + m - 1)
                    c = slice(m * P, (m + 1) * P)
                    three(wops[m % 2][:, 0:2 * P],
                          [(wo_h[:, d, c], wo_l[:, d, c], oh[:, u, d, :], ol[:, u, d, :]) for d in range(2)]
                          ).then_inc(s_f, 1)

            def a_step(i, q, last=False):
                u, j = q // 2, q % 2
                more = not (last and q == 3)
                zz = (lambda *ks: z_part(i, q + 1, ks)) if more else (lambda *ks: None)
                r = q % 2
                before = group_before(i, u)

                def oo(n):
                    if before:
                        out_products(*before, [4 * j + n])

                zz(0, 1)
                wait(pe, s_zl, i, 4, q + 1)
                wait(pe, s_wcl, i, 4, q + 1)
                for c in range(4):
                    d = slice(c * P, (c + 1) * P)
                    e = three(qkps[:, d], [(zh[:, r, d], zl[:, r, d], wch[:, r, 0:P], wcl[:, r, 0:P])])
                e.then_inc(s_qk, 1)
                zz(2, 3)
                oo(0)
                wait(pe, s_qkl, i, 4, q + 1)
                wait(pe, s_ol, i, 4, q)
                three(chps[:, 0:P], [(qkh[:, c, :], qkl[:, c, :], qkh[:, 2 + c, :], qkl[:, 2 + c, :])
                                     for c in range(2)]).then_inc(s_s, 1)
                zz(4, 5)
                oo(1)
                wait(pe, s_p, i, 4, q + 1)
                nc.tensor.transpose(chps[:, 0:P], pn[:, :], ident[:, :]).then_inc(s_t, 1)
                zz(6)
                oo(2)
                wait(pe, s_ptl, i, 4, q + 1)
                three(chps[:, 0:P], [(wch[:, r, P:2 * P], wcl[:, r, P:2 * P], pth[:, :], ptl[:, :])]).then_inc(s_u, 1)
                zz(7)
                oo(3)
                wait(pe, s_ul, i, 4, q + 1)
                for c in range(2):
                    d = slice(2 * DH + c * P, 2 * DH + (c + 1) * P)
                    e = three(chps[:, c * P:(c + 1) * P], [(zh[:, r, d], zl[:, r, d], uh[:, :], ul[:, :])])
                e.then_inc(s_o, 1)

            def a_body(i, last=False):
                for q in range(4):
                    a_step(i, q, last)

            z_part(0, 0, range(K), start_up=True)
            sort_counts()
            a_step(0, 0)
            sort_ranks()
            a_step(0, 1)
            sort_rows()
            pe.wait_ge(s_wl, NCH)
            pe.wait_ge(s_order, 1)
            a_step(0, 2)
            a_step(0, 3)
            with pe.Fori(1, IA - 1) as i:
                a_body(i)
            a_body(IA - 1, last=True)
            out_products(IA - 1, 1, range(K))

            def cond_set(i, q, t, bufs):
                wait(pe, s_yf, i, 16, 4 * q + t - 3)
                x_pair = xs[:, q % 2, :, :]
                for m in range(2):
                    c = slice((2 * t + m) * P, (2 * t + m + 1) * P)
                    y_m = c2ps[t][:, m * 2 * P:(m + 1) * 2 * P]
                    n = P // len(bufs)
                    for h, b in enumerate(bufs):
                        hi = w2[:, b, 0:K * T].rearrange("p (k n) -> p k n", k=K)
                        lo = w2[:, b, K * T:].rearrange("p (k n) -> p k n", k=K)
                        at = slice(h * n, (h + 1) * n)
                        both = y_m.rearrange("p (l n) -> p l n", l=2)[:, :, at]
                        for k in range(K):
                            x_k = x_pair[:, k, :].rearrange("p (l n) -> p l n", l=2)[:, :, at]
                            mm(both, hi[:, k, c], x_k, start=(k == 0), stop=False)
                        for k in range(K):
                            e = mm(y_m[:, at], lo[:, k, c], x_pair[:, k, at], start=False, stop=(k == K - 1))
                e.then_inc(s_c2, 1)

            def gate(i, q):
                u, c = q // 2, slice((q % 2) * P, (q % 2 + 1) * P)
                wait(pe, s_yl, i, 16, 4 * q + 4)
                wait(pe, s_gs, i, 4, q)
                for k in range(K):
                    mm(gps[:, 0:2 * RG], yh[:, u, k, c], ag[:, k, :], start=(k == 0), stop=False)
                for k in range(K):
                    e = mm(gps[:, 0:RG], yl[:, u, k, c], ag[:, k, 0:RG], start=False, stop=(k == K - 1))
                e.then_inc(s_g, 1)

            def transposes(i, u):
                wait(pe, s_m, i, 4, 2 * u + 2)
                for h in range(2):
                    e = nc.tensor.transpose(mtps[:, h * P:(h + 1) * P], mhl[:, h, :], ident16[:, :])
                e.then_inc(s_mt, 1)

            def ffn(i, u, ms):
                for m in ms:
                    wait(pe, s_ft, i, 16, FA + 8 * u + m - 1)
                    c = slice(m * P, (m + 1) * P)
                    dst = fps[m % 2][:, 0:2 * P]
                    three(dst, [(wf_h[:, k, c], wf_l[:, k, c], yh[:, u, k, :], yl[:, u, k, :]) for k in range(K)],
                          last=False)
                    wait(pe, s_mT, i, 2, u + 1)
                    mm(dst, bl_h[:, c], mT[:, :], start=False, stop=False)
                    mm(dst, bl_l[0:R, c], mT[0:R, :], start=False, stop=True).then_inc(s_f, 1)

            def b_step(i, q, first=False):
                u, j = q // 2, q % 2
                pi, pu = (i, 0) if u == 1 else (i - 1, 1)
                before = not (first and u == 0)
                way = pe.value_load(order[0:1, bass.ds(WAY + 4 * i + q, 1)], min_val=0, max_val=3)
                rank = pe.value_load(order[0:1, bass.ds(NEED + 4 * i + q, 1)], min_val=0, max_val=NC - 1)
                pe.wait_ge(s_pw, K * rank + 2 * K)
                wait(pe, s_xl, i, 4, NP + q + 1)

                def conditioned(*bufs):
                    cond_set(i, q, 0, bufs)
                    if q > 0:
                        gate(i, q - 1)
                    elif not first:
                        gate(i - 1, 3)
                    for t in range(1, 4):
                        cond_set(i, q, t, bufs)

                with pe.If(way < 2):
                    with pe.If(way < 1):
                        conditioned(0)
                    with pe.Else():
                        conditioned(1)
                with pe.Else():
                    with pe.If(way < 3):
                        conditioned(0, 1)
                    with pe.Else():
                        conditioned(1, 0)
                if j == 0 and before:
                    transposes(pi, pu)
                if before:
                    ffn(pi, pu, range(4 * j, 4 * j + 4))

            def b_body(i, first=False):
                for q in range(4):
                    b_step(i, q, first)

            pe.wait_ge(s_res, FA)
            pe.wait_ge(s_pw, K)
            pe.sem_inc(s_c2, 1)
            b_body(0, first=True)
            with pe.Fori(1, IB - 1) as i:
                b_body(i)
            b_body(IB - 1)
            gate(IB - 1, 3)
            transposes(IB - 1, 1)
            ffn(IB - 1, 1, range(K))


def kernel(x, itok_B_0_15, L0_cond_weights, L0_attn_Wqkv, L0_attn_bqkv, L0_attn_Wo, L0_attn_bo, L0_cond2_weight,
           L0_ffn_W, L0_ffn_b, L0_ffn_A, L0_ffn_B, L0_ffn_gate_w, L0_ffn_gate_b):
    import numpy as np
    from concourse import bacc
    from concourse.bass_utils import run_bass_kernel_spmd

    a = {n: np.asarray(v) for n, v in locals().items() if n not in ("np", "bacc", "run_bass_kernel_spmd")}
    x = a["x"]
    NB = x.shape[0]

    def chunked(w):
        return np.ascontiguousarray(w.reshape(-1, P, w.shape[1]).transpose(1, 0, 2).reshape(P, -1))

    wc = a["L0_cond_weights"]
    bias = np.concatenate([a[n].reshape(-1, P).T for n in ("L0_attn_bqkv", "L0_attn_bo", "L0_ffn_b")], axis=1)
    bt = a["L0_ffn_B"].T
    arrays = {
        "x_in": x.reshape(NB // 4, 4, S, K, P).transpose(0, 4, 1, 3, 2).reshape(NB // 4, P, GR),
        "ids_in": a["itok_B_0_15"].reshape(1, NB),
        "wc_in": np.stack([wc, wc.transpose(0, 2, 1)], axis=2),
        "wqkv_in": chunked(a["L0_attn_Wqkv"]),
        "wo_in": chunked(a["L0_attn_Wo"]),
        "w2_in": a["L0_cond2_weight"].transpose(0, 2, 1).reshape(NC, K, P, T).transpose(0, 2, 1, 3).reshape(NC, P, K * T),
        "w_in": chunked(a["L0_ffn_W"].T),
        "ag_in": chunked(np.concatenate([a["L0_ffn_A"], a["L0_ffn_gate_w"]], axis=0).T),
        "bl_in": np.concatenate([bt, bt], axis=0),
        "bias_in": bias,
        "gb_in": a["L0_ffn_gate_b"].reshape(1, G4),
    }
    arrays = {n: np.ascontiguousarray(v) for n, v in arrays.items()}
    nc = bacc.Bacc("TRN2", target_bir_lowering=False, num_devices=1)
    args = {n: nc.dram_tensor(n, v.shape, mybir.dt.from_np(v.dtype), kind="ExternalInput").ap()
            for n, v in arrays.items()}
    out = nc.dram_tensor("out", [NB, P, BT], F32, kind="ExternalOutput").ap()
    x1 = nc.dram_tensor("x1", [NB, P, BT], F32, kind="Internal").ap()
    build(nc, NB, out=out, x1=x1, **args)
    r = run_bass_kernel_spmd(nc, [arrays], core_ids=[0])
    got = np.asarray(r.results[0]["out"])
    return np.ascontiguousarray(got.reshape(NB, P, K, S).transpose(0, 3, 2, 1)).reshape(NB, S, T)
```

```python
from contextlib import ExitStack

import concourse.bass as bass
from concourse import mybir

F32, F16, I32 = mybir.dt.float32, mybir.dt.float16, mybir.dt.int32
ALU = mybir.AluOpType
ACT = mybir.ActivationFunctionType
AX = mybir.AxisListType

P = 128
S = 64
T = 1024
K = T // P
DH = 256
NC = 16
R = 64
RANKS = (8, 16, 32, 64)
G4 = len(RANKS)
RG = R + G4
BT = K * S
PT2 = 2 * BT
GR = 2 * PT2
RING = 4
PART = 2
STAGE = 2
PARTS = K // PART

SX = 16.0
SZ = 4.0
SC = 16.0
SW = 256.0
SP = 256.0
SU = 32.0
SO = SZ * SU
SQ = SZ * SC

EXP_SCALE = 1.0 / (SQ * SQ * DH ** 0.5)
MASKED = -1.0e30

B_QK, B_V, B_O, B_F, NBIAS = 0, 4, 6, 14, 22


def wait(eng, sem, i, a, b):
    if isinstance(i, int):
        if a * i + b > 0:
            eng.wait_ge(sem, a * i + b)
    else:
        assert a + b > 0, "the first looped step would wait for nothing: peel it"
        eng.wait_ge(sem, a * i + b)


def build(nc, NB, x_in, ids_in, wc_in, wqkv_in, wo_in, w2_in, w_in, ag_in, bl_in, bias_in, gb_in, out, x1):
    NP = NB // 2
    GA = NP // 2
    IA = GA // 2
    NSL, GB, IB = NP, GA, IA
    assert GA % RING == 0 and NB <= P
    FA = 8 * GA

    ctx = ExitStack()
    with ctx:
        def sb(name, shape, dt):
            return ctx.enter_context(nc.sbuf_tensor(name, shape, dt))

        def sem(name):
            return ctx.enter_context(nc.semaphore(name))

        xr = sb("xr", [P, RING * GR], F32)
        stage = sb("stage", [P, STAGE, PART * T], F32)
        w2 = sb("w2", [P, 2, 2 * K * T], F16)
        wf = sb("wf", [P, 2 * K * T], F16)
        wf_h = wf[:, 0:K * T].rearrange("p (k n) -> p k n", k=K)
        wf_l = wf[:, K * T:].rearrange("p (k n) -> p k n", k=K)
        NQ = 3 * DH
        wa = w2[:, 1, :]
        wq_h = wa[:, 0:K * NQ].rearrange("p (k n) -> p k n", k=K)
        wq_l = wa[:, K * NQ:2 * K * NQ].rearrange("p (k n) -> p k n", k=K)
        o0 = 2 * K * NQ
        wo_h = wa[:, o0:o0 + 2 * T].rearrange("p (k n) -> p k n", k=2)
        wo_l = wa[:, o0 + 2 * T:o0 + 4 * T].rearrange("p (k n) -> p k n", k=2)
        ag = sb("ag", [P, K, 2 * RG], F16)
        bl_h = sb("bl_h", [P, T], F16)
        bl_l = sb("bl_l", [P, T], F16)
        xs = sb("xs", [P, 2, K, 2 * P], F16)
        zh_flat = sb("zh", [P, 2 * NQ], F16)
        zl_flat = sb("zl", [P, 2 * NQ], F16)
        zh = zh_flat[:, :].rearrange("p (r n) -> p r n", r=2)
        zl = zl_flat[:, :].rearrange("p (r n) -> p r n", r=2)
        qkh = sb("qkh", [P, 4, P], F16)
        qkl = sb("qkl", [P, 4, P], F16)
        wcf = sb("wcf", [P, 4, 2 * P], F32)
        wch = sb("wch", [P, 2, 2 * P], F16)
        wcl = sb("wcl", [P, 2, 2 * P], F16)
        sm = sb("sm", [P, P], F32)
        ex = sb("ex", [P, P], F32)
        pn = sb("pn", [P, P], F32)
        soft = sb("soft", [P, 4], F32)
        pth = sb("pth", [P, P], F16)
        ptl = sb("ptl", [P, P], F16)
        uh = sb("uh", [P, P], F16)
        ul = sb("ul", [P, P], F16)
        oh = sb("oh", [P, 2, 2, 2 * P], F16)
        ol = sb("ol", [P, 2, 2, 2 * P], F16)
        ft = sb("ft", [P, 2, 2 * P], F32)
        tt = zh_flat[:, 0:8 * P].bitcast(F32).rearrange("p (r m n) -> p r m n", r=2, m=2)
        yf = zl_flat[:, 0:8 * P].bitcast(F32).rearrange("p (r m n) -> p r m n", r=2, m=2)
        y_flat = sb("y", [P, 8 * K * P], F16)
        yhl = y_flat[:, :].rearrange("p (r k n) -> p r k n", r=2, k=K)
        yh, yl = yhl[:, :, :, 0:2 * P], yhl[:, :, :, 2 * P:4 * P]
        gt = sb("gt", [P, RG], F32)
        gs = sb("gs", [P, 2, RG], F32)
        gb = sb("gb", [P, 2, G4], F32)
        sc = sb("sc", [P, 2, G4], F32)
        pm = sb("pm", [P, 2, 2], F32)
        m012 = sb("m012", [P, 2, 1], F32)
        m123 = sb("m123", [P, 2, 1], F32)
        mx = sb("mx", [P, 2, 1], F32)
        dd = sb("dd", [P, 2, G4], F32)
        ee = sb("ee", [P, 2, G4], F32)
        den = sb("den", [P, 2], F32)
        ptop = sb("ptop", [P, 2], F32)
        itop = sb("itop", [P, 2], F32)
        cw = sb("cw", [P, 2, G4], F32)
        mf = sb("mf", [P, 2, R], F32)
        mhl = sb("mhl", [P, 2, 2 * R], F16)
        mT = sb("mT", [P, 2 * P], F16)
        bias = sb("bias", [P, NBIAS], F32)
        biasq = sb("biasq", [P, 6], F32)
        ident = sb("ident", [P, P], F32)
        ident16 = sb("ident16", [P, P], F16)
        mask = sb("mask", [P, P], F32)
        scratch = y_flat[:, 0:4 * K * P].bitcast(F32)
        taken = [0]

        def carve(rows_, n):
            taken[0] += n
            assert taken[0] <= 2 * K * P
            return scratch[0:rows_, taken[0] - n:taken[0]]

        idc_i = sb("idc_i", [P, 1], I32)
        idr_i = sb("idr_i", [P, NB], I32)
        cols = sb("cols", [P, 3], F32)
        idr = carve(P, NB)
        same = carve(P, NB)
        lower = carve(P, NB)
        iota_s = carve(P, NB)
        hot = carve(P, NB)
        used_b = carve(NC, P)
        rank_hot = carve(NC, NC)
        rows = carve(1, 2 * NB + 3 * NC)
        own = sb("own", [P, NC], F32)
        ones = sb("ones", [P, P], F32)
        tri = sb("tri", [NC, 2 * NC], F32)
        iota_e = sb("iota_e", [P, NC], F32)
        place = sb("place", [P, 1], F32)
        per_c = sb("per_c", [NC, 5], F32)
        rank_c = sb("rank_c", [NC, 1], F32)
        ab = sb("ab", [1, 2 * NSL], I32)
        late = sb("late", [1, 2], F32)
        order = sb("order", [1, NB + 2 * NSL + 2 * NC + 2], I32)
        SRC, WAY, NEED, LIST, THRU = 0, NB, NB + NSL, NB + 2 * NSL, NB + 2 * NSL + NC
        BEGIN = THRU + NC

        bank = [ctx.enter_context(nc.psum_tensor(f"bank{n}", [P, 512], F32)) for n in range(8)]
        zps = [[bank[0], bank[1]], [bank[2], bank[3]]]
        qkps, chps, wops = bank[4], bank[5], [bank[6], bank[7]]
        c2ps, fps, gps, trps = bank[0:4], [bank[4], bank[5]], bank[6], bank[7]
        mtps = trps[:, 0:P].bitcast(F16)

        s_ids, s_bias, s_gb = sem("ids_loaded"), sem("biases_loaded"), sem("gate_bias_loaded")
        s_x_first = sem("x_of_pair_0_loaded")
        s_pst = [sem(f"pool_stage{n}_loaded") for n in range(STAGE)]
        s_wh, s_wl = sem("weight_hi_made"), sem("weight_lo_made")
        s_pc, s_pw = sem("pool_hi_scaled"), sem("pool_chunk_made")
        s_cst, s_pm0, s_zero = sem("constants_made"), sem("pool_memsets"), sem("zeros_made")
        s_bq = sem("scaled_biases")
        s_sort, s_sp = sem("sort_step"), sem("sort_products")
        s_order = sem("order_ready")
        s_x = [sem("x_even_loaded"), sem("x_odd_loaded")]
        s_st = [sem("x1_even_stored"), sem("x1_odd_stored")]
        s_last = sem("x1_last_stored")
        s_out = [sem("out_even_stored"), sem("out_odd_stored")]
        s_wc = [sem(f"mix{n}_loaded") for n in range(4)]
        s_xh, s_xl = sem("x_hi"), sem("x_lo")
        s_z, s_zh, s_zl = sem("z_done"), sem("z_hi"), sem("z_lo")
        s_wch, s_wcl = sem("mix_hi"), sem("mix_lo")
        s_qk, s_qkh, s_qkl = sem("qk_done"), sem("qk_hi"), sem("qk_lo")
        s_s, s_sm, s_e = sem("scores_done"), sem("scores_masked"), sem("exp_done")
        s_r, s_p = sem("sum_inverted"), sem("probs_ready")
        s_t, s_pth, s_ptl = sem("probs_transposed"), sem("pt_hi"), sem("pt_lo")
        s_u, s_uh, s_ul = sem("u_done"), sem("u_hi"), sem("u_lo")
        s_o, s_oh, s_ol = sem("o_done"), sem("o_hi"), sem("o_lo")
        s_fs = sem("ffn_chunk_summed")
        s_f, s_ft, s_res = sem("out_chunk_done"), sem("out_chunk_biased"), sem("out_chunk_residual")
        s_turn_sp, s_turn_dve, s_turn_pool = sem("sp_turns"), sem("dve_turns"), sem("pool_turns")
        s_c2, s_tt, s_yf = sem("y_set_done"), sem("y_hilo_copied"), sem("y_summed")
        s_yh, s_yl = sem("y_hi"), sem("y_lo")
        s_g, s_gt, s_gs = sem("gate_done"), sem("gate_hilo_copied"), sem("gate_summed")
        s_chain, s_dd, s_ee, s_m = sem("gating_step"), sem("gate_shifted"), sem("gate_exp"), sem("middle_ready")
        s_mt, s_mT = sem("middle_transposed"), sem("middle_copied")

        early = w2[:, 0, :].bitcast(F32)
        chunks = []
        for k in range(K):
            chunks.append((wqkv_in[:, k * NQ:(k + 1) * NQ], early[:, k * NQ:(k + 1) * NQ], wq_h[:, k, :], wq_l[:, k, :]))
        for k in range(2):
            chunks.append((wo_in[:, k * T:(k + 1) * T], early[:, K * NQ + k * T:K * NQ + (k + 1) * T],
                           wo_h[:, k, :], wo_l[:, k, :]))
        chunks.append((ag_in.rearrange("p (k n) -> p k n", k=K), stage[:, 0, 0:K * RG].rearrange("p (k n) -> p k n", k=K),
                       ag[:, :, 0:RG], ag[:, :, RG:2 * RG]))
        chunks.append((bl_in, stage[:, 1, 0:T], bl_h[:, :], bl_l[:, :]))
        NCH = len(chunks)
        s_chunk = [sem(f"chunk{n}_loaded") for n in range(NCH)]

        def group_cols(g, lo=0, n=GR):
            return xr[:, bass.ds((g % RING) * GR + lo, n)]

        def batch_view(i, q, b):
            v = group_cols(2 * i + q // 2, (q % 2) * PT2 + b * BT, BT)
            return v.rearrange("p (k s) -> p k s", k=K)

        def split_view(q, b, half):
            return xs[:, q % 2, :, half * P + b * S:half * P + (b + 1) * S]

        def chunk_view(g, m):
            return group_cols(g).rearrange("p (b k s) -> p b k s", b=4, k=K)[:, :, m, :]

        def group_before(i, u):
            if u == 1:
                return i, 0
            return None if isinstance(i, int) and i == 0 else (i - 1, 1)

        def out_share(q, n, last):
            if last and q >= 2:
                return [] if q == 2 else [2 * n, 2 * n + 1]
            return [4 * (q % 2) + n]

        def x_ready(eng, i, q, phase_b):
            u = (q // 2) % 2
            n = q // 4
            if phase_b:
                wait(eng, s_x[u], i, 64, 16 * IA + 64 * (n + 1))
            elif isinstance(i, int) and i == 0 and q == 0:
                eng.wait_ge(s_x_first, 16)
            else:
                wait(eng, s_x[u], i, 16, 16 * (n + 1))

        block = ctx.enter_context(nc.Block())

        @block.sync
        def _(sp):
            def load_x(i, u):
                sp.dma_start(group_cols(2 * i + u), x_in[bass.ds(2 * i + u, 1), :, :].rearrange("a p n -> (a p) n")
                             ).then_inc(s_x[u], 16)

            def load_mix(i, q):
                n = q % 4
                wait(sp, s_wcl, i, 4, q - 3)
                sp.sem_inc(s_turn_sp, 1)
                for b in range(2):
                    e = sp.value_load(idr_i[0:1, bass.ds(8 * i + 2 * q + b, 1)], min_val=0, max_val=NC - 1)
                    dst = wcf[b * S:(b + 1) * S, n, :].rearrange("p (t d) -> p t d", t=2)[:, :, b * S:(b + 1) * S]
                    src = wc_in[bass.ds(e, 1), :, :, :].rearrange("a c t d -> (a c) t d")
                    sp.dma_start(dst, src).then_inc(s_wc[n], 16)

            def load_chunk(n):
                src, dst, _, _ = chunks[n]
                sp.dma_start(dst, src).then_inc(s_chunk[n], 16)

            def store_x1(i, u):
                wait(sp, s_res, i, 16, 8 * (u + 1))
                sp.sem_inc(s_turn_sp, 1)
                sp.dma_start(x1[bass.ds(4 * (2 * i + u), 4), :, :].rearrange("b p n -> p b n"),
                             group_cols(2 * i + u).rearrange("p (b n) -> p b n", b=4)).then_inc(s_st[u], 16)

            def batches(i, u):
                return [sp.value_load(order[0:1, bass.ds(SRC + 4 * (2 * i + u) + b, 1)], min_val=0, max_val=NB - 1)
                        for b in range(4)]

            sp.dma_start(idr_i[:, :], ids_in.to_broadcast([P, NB])).then_inc(s_ids, 16)
            sp.dma_start(idc_i[0:NB, :], ids_in.rearrange("a b -> b a")).then_inc(s_ids, 16)
            sp.dma_start(group_cols(0, 0, PT2), x_in[0, :, 0:PT2]).then_inc(s_x_first, 16)
            for n in range(2):
                load_chunk(n)
            sp.dma_start(bias[:, :], bias_in).then_inc(s_bias, 16)
            for n in range(2, 5):
                load_chunk(n)
            sp.dma_start(group_cols(0, PT2, PT2), x_in[0, :, PT2:GR]).then_inc(s_x[0], 16)
            sp.wait_ge(s_ids, 32)
            sp.wait_ge(s_zero, 1)
            load_chunk(5)
            load_mix(0, 0)
            for n in range(6, K):
                load_chunk(n)
            load_mix(0, 1)
            for n in range(K, NCH):
                load_chunk(n)
            for h in range(2):
                sp.dma_start(gb[:, h, :], gb_in.to_broadcast([P, G4])).then_inc(s_gb, 16)
            load_x(0, 1)

            def body(i, first=False, last=False):
                for u in range(2):
                    if not last:
                        wait(sp, s_st[u], i, 16, 0)
                        sp.sem_inc(s_turn_sp, 1)
                        wait(sp, s_x[u], i, 16, 16)
                        sp.sem_inc(s_turn_sp, 1)
                        load_x(i + 1, u)
                    for j in range(2):
                        q = 2 * u + j
                        if not (last and q >= 2):
                            load_mix(i, q + 2)
                    if u == 1:
                        store_x1(i, 0)
                    elif not first:
                        store_x1(i - 1, 1)

            body(0, first=True)
            with sp.Fori(1, IA - 1) as i:
                body(i)

            sp.wait_ge(s_order, 1)
            firsts = [batches(0, u) for u in range(2)]
            begin_even, begin_last = [sp.value_load(order[0:1, BEGIN + n:BEGIN + n + 1], min_val=1,
                                                    max_val=16 * IA + 33) for n in range(2)]
            sp.wait_ge(s_st[0], 16 * (IA - 1))
            body(IA - 1, last=True)

            def load_slots(i, u, rs):
                for b, r in enumerate(rs):
                    sp.dma_start(group_cols(2 * i + u, b * BT, BT),
                                 x1[bass.ds(r, 1), :, :].rearrange("a p n -> (a p) n")).then_inc(s_x[u], 16)

            def store_out(i, u):
                rs = batches(i, u)
                wait(sp, s_res, i, 16, FA + 8 * (u + 1))
                sp.sem_inc(s_turn_sp, 1)
                for b, r in enumerate(rs):
                    sp.dma_start(out[bass.ds(r, 1), :, :].rearrange("a p n -> (a p) n"),
                                 group_cols(2 * i + u, b * BT, BT)).then_inc(s_out[u], 16)

            sp.wait_ge(s_st[1], 16 * (IA - 1))
            sp.wait_ge(s_st[0], begin_even)
            sp.sem_inc(s_turn_sp, 1)
            sp.wait_ge(s_last, begin_last)
            sp.sem_inc(s_turn_sp, 1)
            load_slots(0, 0, firsts[0])
            sp.wait_ge(s_st[0], 16 * IA)
            sp.wait_ge(s_last, 33)
            load_slots(0, 1, firsts[1])

            def body_b(i, first=False, last=False):
                for u in range(2):
                    if not last:
                        rs = batches(i + 1, u)
                        wait(sp, s_out[u], i, 64, 0)
                        sp.sem_inc(s_turn_sp, 1)
                        wait(sp, s_x[u], i, 64, 16 * IA + 64)
                        sp.sem_inc(s_turn_sp, 1)
                        load_slots(i + 1, u, rs)
                    if u == 1:
                        store_out(i, 0)
                    elif not first:
                        store_out(i - 1, 1)

            body_b(0, first=True)
            with sp.Fori(1, IB - 1) as i:
                body_b(i)
            body_b(IB - 1, last=True)
            store_out(IB - 1, 1)
            for u in range(2):
                sp.wait_ge(s_out[u], 64 * IB)

        @block.gpsimd
        def _(pool):
            pool.memset(ident[:, :], 0.0).then_inc(s_pm0, 1)
            pool.memset(ones[:, :], 1.0).then_inc(s_pm0, 1)
            pool.memset(per_c[:, 2:3], 1.0).then_inc(s_pm0, 1)
            pool.iota(cols[:, 0:1], pattern=[[0, 1]], base=0, channel_multiplier=1,
                      allow_small_or_imprecise_dtypes=True).then_inc(s_cst, 1)
            pool.iota(iota_e[:, :], pattern=[[1, NC]], base=0, channel_multiplier=0,
                      allow_small_or_imprecise_dtypes=True).then_inc(s_cst, 1)
            pool.iota(iota_s[:, :], pattern=[[1, NB]], base=0, channel_multiplier=0,
                      allow_small_or_imprecise_dtypes=True).then_inc(s_cst, 1)
            pool.iota(per_c[:, 0:1], pattern=[[0, 1]], base=0, channel_multiplier=1,
                      allow_small_or_imprecise_dtypes=True).then_inc(s_cst, 1)
            pool.wait_ge(s_pm0, 3)
            pool.affine_select(out=lower[:, :], in_=ones[:, 0:NB], compare_op=ALU.is_gt, fill=0.0, base=0,
                               pattern=[[-1, NB]], channel_multiplier=1).then_inc(s_cst, 1)
            pool.wait_ge(s_cst, 5)
            pool.affine_select(out=tri[:, 0:NC], in_=ones[0:NC, 0:NC], compare_op=ALU.is_gt, fill=0.0, base=0,
                               pattern=[[1, NC]], channel_multiplier=-1).then_inc(s_cst, 1)
            pool.wait_ge(s_cst, 6)
            pool.affine_select(out=tri[:, NC:2 * NC], in_=ones[0:NC, 0:NC], compare_op=ALU.is_ge, fill=0.0, base=0,
                               pattern=[[1, NC]], channel_multiplier=-1).then_inc(s_cst, 1)
            pool.wait_ge(s_cst, 7)
            pool.affine_select(out=ident[:, :], in_=ident[:, :], compare_op=ALU.not_equal, fill=1.0, base=0,
                               pattern=[[-1, P]], channel_multiplier=1).then_inc(s_cst, 1)
            pool.wait_ge(s_cst, 8)
            pool.tensor_copy(ident16[:, :], ident[:, :]).then_inc(s_cst, 1)

            def load(src, st):
                pool.dma_start(stage[:, st, :], src).then_inc(s_pst[st], 16)

            def split(hi, lo, t, reload):
                for k in range(PARTS):
                    n = PARTS * t + k
                    pool.wait_ge(s_pst[k % STAGE], 16 * (PARTS // STAGE) * t + 16 * (k // STAGE + 1))
                    pool.sem_inc(s_turn_pool, 1)
                    chunk = [(stage[:, k % STAGE, h * T:(h + 1) * T], slice((k * PART + h) * T, (k * PART + h + 1) * T))
                             for h in range(PART)]
                    for st, c in chunk:
                        pool.tensor_scalar(hi[:, c], st, SW, 1.0, ALU.mult, ALU.mult).then_inc(s_pc, 1)
                        pool.tensor_scalar(st, st, SW, 1.0, ALU.mult, ALU.mult).then_inc(s_pc, 1)
                    for h, (st, c) in enumerate(chunk):
                        pool.wait_ge(s_pc, 2 * (PART * n + h + 1))
                        pool.tensor_tensor(lo[:, c], st, hi[:, c], ALU.subtract).then_inc(s_pw, 1)
                    pool.wait_ge(s_pw, PART * (n + 1))
                    reload(k)

            def reloader(here, after):
                def reload(k):
                    if k < PARTS - STAGE:
                        here(k + STAGE)
                    else:
                        after(k + STAGE - PARTS)
                return reload

            def load_w(k):
                load(w_in[:, k * PART * T:(k + 1) * PART * T], k % STAGE)

            def load_w2(r):
                def part(k):
                    pool.sem_inc(s_turn_pool, 1)
                    e = pool.value_load(order[0:1, bass.ds(LIST + r, 1)], min_val=0, max_val=NC - 1)
                    load(w2_in[bass.ds(e, 1), :, k * PART * T:(k + 1) * PART * T].rearrange("a p n -> (a p) n"),
                         k % STAGE)
                return part

            pool.wait_ge(s_wl, NCH)
            pool.wait_ge(s_order, 1)
            for k in range(STAGE):
                load_w(k)
            split(wf[:, 0:K * T], wf[:, K * T:], 0, reloader(load_w, load_w2(0)))

            def condition(i, b, more=True):
                r = 2 * i + b
                after = load_w2(r + 1) if more else lambda k: None
                split(w2[:, b, 0:K * T], w2[:, b, K * T:], r + 1, reloader(load_w2(r), after))

            def free_buffer(i, b):
                n = pool.value_load(order[0:1, bass.ds(THRU + 2 * i + b - 2, 1)], min_val=0, max_val=NSL)
                pool.wait_ge(s_c2, 4 * n + 1)
                pool.sem_inc(s_turn_pool, 1)

            condition(0, 0)
            pool.wait_ge(s_f, FA)
            condition(0, 1)
            with pool.Fori(1, NC // 2 - 1) as i:
                for b in range(2):
                    free_buffer(i, b)
                    condition(i, b)
            i = NC // 2 - 1
            free_buffer(i, 0)
            condition(i, 0)
            free_buffer(i, 1)
            condition(i, 1, more=False)

        @block.scalar
        def _(act):
            Copy, Iden = ACT.Copy, ACT.Identity

            def x_hi(i, q, phase_b=False):
                x_ready(act, i, q, phase_b)
                for b in range(2):
                    last = nc.scalar.activation(split_view(q, b, 0), batch_view(i, q, b), Copy, scale=SX)
                last.then_inc(s_xh, 1)

            def mix_hi(i, q):
                wait(act, s_wc[q % 4], i, 32, 32 * (q // 4 + 1))
                wait(act, s_u, i, 4, q - 1)
                nc.scalar.activation(wch[:, q % 2, :], wcf[:, q % 4, :], Copy, scale=SC).then_inc(s_wch, 1)

            def chunk_hi(n):
                _, src, hi, _ = chunks[n]
                act.wait_ge(s_chunk[n], 16)
                nc.scalar.activation(hi, src, Copy, scale=SW).then_inc(s_wh, 1)

            x_hi(0, 0)
            for n in range(K):
                chunk_hi(n)
                if n == 5:
                    mix_hi(0, 0)
                if n == 6:
                    x_hi(0, 1)
            for n in (K, K + 1):
                chunk_hi(n)

            def out_chunks(i, u, ms, phase_b=False):
                n0 = FA if phase_b else 0
                for m in ms:
                    wait(act, s_f, i, 16, n0 + 8 * u + m + 1)
                    wait(act, s_res, i, 16, n0 + 8 * u + m - 1)
                    if phase_b:
                        src, b0, scale = fps[m % 2][:, 2 * P:4 * P], B_F, 1.0 / (SX * SW)
                    else:
                        src, b0, scale = wops[m % 2][:, 0:2 * P], B_O, 1.0 / (SO * SW)
                    nc.scalar.activation(ft[:, m % 2, :], src, Iden, bias=bias[:, b0 + m:b0 + m + 1],
                                         scale=scale).then_inc(s_ft, 1)

            def z_hi(i, q):
                wait(act, s_z, i, 4, q + 1)
                for h in range(2):
                    e = nc.scalar.activation(zh[:, q % 2, h * 384:(h + 1) * 384], zps[q % 2][h][:, 0:384], Copy,
                                             scale=SZ / (SX * SW))
                e.then_inc(s_zh, 1)

            def a_step(i, q, last=False):
                u, j = q // 2, q % 2
                before = group_before(i, u)

                def oo(n):
                    if before:
                        out_chunks(*before, out_share(q, n, last))

                wait(act, s_qk, i, 4, q + 1)
                for c in range(4):
                    e = nc.scalar.activation(qkh[:, c, :], qkps[:, c * P:(c + 1) * P], Iden, bias=biasq[:, c:c + 1])
                e.then_inc(s_qkh, 1)
                if not (last and q == 3):
                    mix_hi(i, q + 1)
                oo(0)
                wait(act, s_sm, i, 4, q + 1)
                nc.scalar.activation(ex[:, :], sm[:, :], ACT.Exp, bias=soft[:, 0:1], scale=-1.0,
                                     accum_out=soft[:, 1:2]).then_inc(s_e, 1)
                if not (last and q >= 2):
                    x_hi(i, q + 2)
                oo(1)
                wait(act, s_t, i, 4, q + 1)
                nc.scalar.copy(pth[:, :], chps[:, 0:P]).then_inc(s_pth, 1)
                oo(2)
                wait(act, s_u, i, 4, q + 1)
                nc.scalar.activation(uh[:, :], chps[:, 0:P], Copy, scale=SU / (SC * SP)).then_inc(s_uh, 1)
                if not (last and q == 3):
                    z_hi(i, q + 1)
                oo(3)
                wait(act, s_o, i, 4, q + 1)
                for c in range(2):
                    e = nc.scalar.activation(oh[:, u, c, j * P:(j + 1) * P], chps[:, c * P:(c + 1) * P], Iden,
                                             bias=biasq[:, 4 + c:5 + c])
                e.then_inc(s_oh, 1)

            def a_body(i, last=False):
                for q in range(4):
                    a_step(i, q, last)

            act.wait_ge(s_bias, 16)
            nc.scalar.activation(biasq[:, 0:4], bias[:, B_QK:B_QK + 4], Copy, scale=SQ).then_inc(s_bq, 1)
            nc.scalar.activation(biasq[:, 4:6], bias[:, B_V:B_V + 2], Copy, scale=SO).then_inc(s_bq, 1)
            act.wait_ge(s_bq, 2)
            z_hi(0, 0)
            for q in range(4):
                a_step(0, q)
                if q == 1:
                    chunk_hi(K + 2)
                    chunk_hi(K + 3)
            with act.Fori(1, IA - 1) as i:
                a_body(i)
            a_body(IA - 1, last=True)
            last_g = group_cols(GA - 1).rearrange("p (b n) -> p b n", b=4)

            def store_half(h):
                act.wait_ge(s_res, FA - 4 + 4 * h)
                n = slice(h * BT // 2, (h + 1) * BT // 2)
                act.dma_start(x1[NB - 4:NB, :, n].rearrange("b p n -> p b n"), last_g[:, :, n]).then_inc(s_last, 16)

            act.sem_inc(s_last, 1)
            out_chunks(IA - 1, 1, range(6))
            store_half(0)
            out_chunks(IA - 1, 1, range(6, K))
            store_half(1)

            def y_set(i, q, t):
                wait(act, s_c2, i, 16, 4 * q + t + 2)
                wait(act, s_yf, i, 16, 4 * q + t - 1)
                src = c2ps[t][:, :].rearrange("p (m h n) -> p m h n", m=2, h=2)
                nc.scalar.activation(tt[:, t % 2, :, :], src[:, :, 1, :], Copy, scale=1.0 / SW).then_inc(s_tt, 1)
                wait(act, s_yf, i, 16, 4 * q + t + 1)
                nc.scalar.copy(yh[:, q // 2, 2 * t:2 * t + 2, (q % 2) * P:(q % 2 + 1) * P], yf[:, t % 2, :, :]
                               ).then_inc(s_yh, 1)

            def gate_copy(i, q):
                wait(act, s_g, i, 4, q + 1)
                wait(act, s_gs, i, 4, q)
                nc.scalar.copy(gt[:, :], gps[:, RG:2 * RG]).then_inc(s_gt, 1)

            def gate_exp(i, u):
                wait(act, s_dd, i, 2, u + 1)
                nc.scalar.activation(ee[:, :, :], dd[:, :, :], ACT.Exp).then_inc(s_ee, 1)

            def middle_copy(i, u):
                wait(act, s_mt, i, 2, u + 1)
                nc.scalar.copy(mT[:, :], mtps).then_inc(s_mT, 1)

            def b_step(i, q, first=False, last=False):
                u, j = q // 2, q % 2
                pi, pu = (i, 0) if u == 1 else (i - 1, 1)
                y_set(i, q, 0)
                if q > 0:
                    gate_copy(i, q - 1)
                elif not first:
                    gate_copy(i - 1, 3)
                before = not (first and u == 0)
                if j == 0 and before:
                    gate_exp(pi, pu)
                y_set(i, q, 1)
                if not (last and q == 3):
                    x_hi(i, q + 1, phase_b=True)
                y_set(i, q, 2)
                y_set(i, q, 3)
                if j == 0 and before:
                    middle_copy(pi, pu)
                if before:
                    out_chunks(pi, pu, range(4 * j, 4 * j + 4), phase_b=True)

            def b_body(i, first=False, last=False):
                for q in range(4):
                    b_step(i, q, first, last)

            x_hi(0, 0, phase_b=True)
            b_body(0, first=True)
            with act.Fori(1, IB - 1) as i:
                b_body(i)
            b_body(IB - 1, last=True)
            gate_copy(IB - 1, 3)
            gate_exp(IB - 1, 1)
            middle_copy(IB - 1, 1)
            out_chunks(IB - 1, 1, range(K), phase_b=True)

        @block.vector
        def _(dve):
            v = nc.vector
            v.memset(wcf[:, :, :], 0.0).then_inc(s_zero, 1)
            for a in range(2):
                for b in range(2):
                    v.memset(mask[a * S:(a + 1) * S, b * S:(b + 1) * S], 0.0 if a == b else MASKED).then_inc(s_zero, 1)

            done = [0]

            def link(ins):
                done[0] += 1
                ins.then_inc(s_sort, 1)
                dve.wait_ge(s_sort, done[0])

            dve.wait_ge(s_ids, 32)
            dve.wait_ge(s_cst, 9)
            dve.wait_ge(s_zero, 5)
            link(v.tensor_copy(cols[0:NB, 2:3], idc_i[0:NB, :]))
            link(v.tensor_copy(idr[0:NB, :], idr_i[0:NB, :]))
            link(v.tensor_scalar(own[0:NB, :], iota_e[0:NB, :], cols[0:NB, 2:3], None, ALU.is_equal))
            link(v.tensor_scalar(same[0:NB, :], idr[0:NB, :], cols[0:NB, 2:3], None, ALU.is_equal))
            link(v.tensor_tensor(same[0:NB, :], same[0:NB, :], lower[0:NB, :], ALU.mult))
            link(v.tensor_scalar(idr[0:NB, :], idr[0:NB, :], cols[0:NB, 2:3], None, ALU.is_lt))
            link(v.tensor_tensor_reduce(out=idr[0:NB, :], in0=idr[0:NB, :], in1=same[0:NB, :], scale=1.0, scalar=0.0,
                                        op0=ALU.add, op1=ALU.add, accum_out=place[0:NB, :]))
            link(v.tensor_scalar(hot[0:NB, :], iota_s[0:NB, :], place[0:NB, :], None, ALU.is_equal))

            def count_conditions():
                dve.wait_ge(s_sp, 1)
                link(v.tensor_copy(per_c[:, 3:4], trps[0:NC, 0:1]))
                link(v.tensor_scalar(per_c[:, 4:5], per_c[:, 3:4], 1.0, None, ALU.min))
                link(v.tensor_scalar(used_b[:, :], ones[0:NC, :], per_c[:, 4:5], None, ALU.mult))

            def rank_conditions():
                dve.wait_ge(s_sp, 2)
                link(v.tensor_tensor_reduce(out=own[0:NB, :], in0=own[0:NB, :], in1=trps[0:NB, 0:NC], scale=1.0,
                                            scalar=0.0, op0=ALU.mult, op1=ALU.add, accum_out=cols[0:NB, 1:2]))
                link(v.tensor_copy(rank_c[:, :], trps[0:NC, NC:NC + 1]))
                link(v.tensor_copy(per_c[:, 1:2], trps[0:NC, NC + 1:NC + 2]))
                link(v.tensor_scalar(rank_hot[:, :], iota_e[0:NC, :], rank_c[:, :], per_c[:, 4:5], ALU.is_equal,
                                     ALU.mult))

            def take_rows():
                dve.wait_ge(s_sp, 3)
                link(v.tensor_copy(rows[:, :], trps[0:1, 0:2 * NB + 3 * NC]))

            def write_order():
                link(v.tensor_copy(order[0:1, SRC:SRC + NB], rows[:, 0:NB]))
                link(v.tensor_copy(order[0:1, LIST:LIST + NC], rows[:, 2 * NB:2 * NB + NC]))
                link(v.tensor_tensor(late[:, :], rows[:, 0:2], rows[:, 2:4], ALU.max))
                link(v.tensor_tensor(late[:, 0:1], late[:, 0:1], late[:, 1:2], ALU.max))
                for n, (each, least) in enumerate(((16, 16 * (IA - 1)), (32, 1))):
                    link(v.tensor_scalar(late[:, 1:2], late[:, 0:1], float(NB - 8), float(each), ALU.is_ge, ALU.mult))
                    link(v.tensor_scalar(order[0:1, BEGIN + n:BEGIN + n + 1], late[:, 1:2], float(least), None, ALU.add))
                upto = rows[:, 2 * NB + NC:2 * NB + 2 * NC]
                occurs = rows[:, 2 * NB + 2 * NC:2 * NB + 3 * NC]
                link(v.scalar_tensor_tensor(out=upto, in0=occurs, scalar=-float(NB), in1=upto, op0=ALU.mult, op1=ALU.add))
                link(v.tensor_scalar(order[0:1, THRU:THRU + NC], upto, float(NB + 1), None, ALU.add))
                link(v.tensor_scalar(order[0:1, THRU:THRU + NC], order[0:1, THRU:THRU + NC], 1, None,
                                     ALU.logical_shift_right))
                two = rows[:, NB:2 * NB].rearrange("p (s h) -> p s h", h=2)
                first, second = ab[:, 0:NSL], ab[:, NSL:2 * NSL]
                link(v.tensor_copy(first, two[:, :, 0]))
                link(v.tensor_copy(order[0:1, NEED:NEED + NSL], two[:, :, 1]))
                link(v.tensor_scalar(first, first, 1, None, ALU.bitwise_and))
                link(v.tensor_tensor(second, two[:, :, 1], two[:, :, 0], ALU.subtract))
                link(v.tensor_scalar(second, second, 1, None, ALU.logical_shift_left))
                v.tensor_tensor(order[0:1, WAY:WAY + NSL], first, second, ALU.bitwise_or).then_inc(s_order, 1)

            def x_lo(i, q, b, phase_b=False):
                x_ready(dve, i, q, phase_b)
                wait(dve, s_xh, i, 4, (NP if phase_b else 0) + q + 1)
                e = v.scalar_tensor_tensor(out=split_view(q, b, 1), in0=batch_view(i, q, b), scalar=SX,
                                           in1=split_view(q, b, 0), op0=ALU.mult, op1=ALU.subtract)
                if b == 1:
                    e.then_inc(s_xl, 1)

            def mix_lo(i, q):
                wait(dve, s_wch, i, 4, q + 1)
                v.scalar_tensor_tensor(out=wcl[:, q % 2, :], in0=wcf[:, q % 4, :], scalar=SC, in1=wch[:, q % 2, :],
                                       op0=ALU.mult, op1=ALU.subtract).then_inc(s_wcl, 1)

            def chunk_lo(n):
                _, src, hi, lo = chunks[n]
                dve.wait_ge(s_wh, n + 1)
                v.scalar_tensor_tensor(out=lo, in0=src, scalar=SW, in1=hi, op0=ALU.mult,
                                       op1=ALU.subtract).then_inc(s_wl, 1)

            sort_parts = (count_conditions, rank_conditions, take_rows)
            for b in range(2):
                x_lo(0, 0, b)
            for n in range(K):
                chunk_lo(n)
                if n < len(sort_parts):
                    sort_parts[n]()
                if n == 5:
                    mix_lo(0, 0)
                if n == 6:
                    for b in range(2):
                        x_lo(0, 1, b)
            for n in (K, K + 1):
                chunk_lo(n)

            def residual(i, u, ms, phase_b=False):
                n0 = FA if phase_b else 0
                for m in ms:
                    wait(dve, s_ft, i, 16, n0 + 8 * u + m + 1)
                    if phase_b:
                        v.scalar_tensor_tensor(out=ft[:, m % 2, :], in0=fps[m % 2][:, 0:2 * P], scalar=1.0 / (SX * SW),
                                               in1=ft[:, m % 2, :], op0=ALU.mult, op1=ALU.add).then_inc(s_fs, 1)
                        wait(dve, s_fs, i, 16, 8 * u + m + 1)
                    ring = chunk_view(2 * i + u, m)
                    v.tensor_tensor(ring, ft[:, m % 2, :].rearrange("p (b s) -> p b s", b=4), ring,
                                    ALU.add).then_inc(s_res, 1)

            def z_lo(i, q):
                wait(dve, s_zh, i, 4, q + 1)
                for h in range(2):
                    c = slice(h * 384, (h + 1) * 384)
                    e = v.scalar_tensor_tensor(out=zl[:, q % 2, c], in0=zps[q % 2][h][:, 0:384],
                                               scalar=SZ / (SX * SW), in1=zh[:, q % 2, c], op0=ALU.mult,
                                               op1=ALU.subtract)
                e.then_inc(s_zl, 1)

            def a_step(i, q, last=False):
                u, j = q // 2, q % 2
                before = group_before(i, u)

                def oo(n):
                    if before:
                        residual(*before, out_share(q, n, last))

                wait(dve, s_qkh, i, 4, q + 1)
                for c in range(4):
                    e = v.scalar_tensor_tensor(out=qkl[:, c, :], in0=qkps[:, c * P:(c + 1) * P],
                                               scalar=biasq[:, c:c + 1], in1=qkh[:, c, :], op0=ALU.add,
                                               op1=ALU.subtract)
                e.then_inc(s_qkl, 1)
                if not (last and q == 3):
                    mix_lo(i, q + 1)
                oo(0)
                wait(dve, s_s, i, 4, q + 1)
                dve.sem_inc(s_turn_dve, 1)
                v.tensor_tensor_reduce(out=sm[:, :], in0=chps[:, 0:P], in1=mask[:, :], scale=-EXP_SCALE,
                                       scalar=3.0e38, op0=ALU.add, op1=ALU.min,
                                       accum_out=soft[:, 0:1]).then_inc(s_sm, 1)
                wait(dve, s_e, i, 4, q + 1)
                v.reciprocal(soft[:, 2:3], soft[:, 1:2]).then_inc(s_r, 1)
                wait(dve, s_r, i, 4, q + 1)
                v.tensor_scalar(pn[:, :], ex[:, :], soft[:, 2:3], SP, ALU.mult, ALU.mult).then_inc(s_p, 1)
                if not (last and q >= 2):
                    x_lo(i, q + 2, 0)
                oo(1)
                wait(dve, s_pth, i, 4, q + 1)
                v.tensor_tensor(ptl[:, :], chps[:, 0:P], pth[:, :], ALU.subtract).then_inc(s_ptl, 1)
                if not (last and q >= 2):
                    x_lo(i, q + 2, 1)
                oo(2)
                wait(dve, s_uh, i, 4, q + 1)
                v.scalar_tensor_tensor(out=ul[:, :], in0=chps[:, 0:P], scalar=SU / (SC * SP), in1=uh[:, :],
                                       op0=ALU.mult, op1=ALU.subtract).then_inc(s_ul, 1)
                if not (last and q == 3):
                    z_lo(i, q + 1)
                oo(3)
                wait(dve, s_oh, i, 4, q + 1)
                for c in range(2):
                    e = v.scalar_tensor_tensor(out=ol[:, u, c, j * P:(j + 1) * P], in0=chps[:, c * P:(c + 1) * P],
                                               scalar=biasq[:, 4 + c:5 + c], in1=oh[:, u, c, j * P:(j + 1) * P],
                                               op0=ALU.add, op1=ALU.subtract)
                e.then_inc(s_ol, 1)

            def a_body(i, last=False):
                for q in range(4):
                    a_step(i, q, last)

            z_lo(0, 0)
            for q in range(4):
                a_step(0, q)
                if q == 1:
                    chunk_lo(K + 2)
                    chunk_lo(K + 3)
                if q == 2:
                    write_order()
            with dve.Fori(1, IA - 1) as i:
                a_body(i)
            a_body(IA - 1, last=True)
            residual(IA - 1, 1, range(K))

            dve.wait_ge(s_gb, 32)

            def y_set(i, q, t):
                wait(dve, s_yl, i, 16, 4 * q + t - 1)
                wait(dve, s_tt, i, 16, 4 * q + t + 1)
                src = c2ps[t][:, :].rearrange("p (m h n) -> p m h n", m=2, h=2)
                v.scalar_tensor_tensor(out=yf[:, t % 2, :, :], in0=src[:, :, 0, :], scalar=1.0 / SW, in1=tt[:, t % 2, :, :],
                                       op0=ALU.mult, op1=ALU.add).then_inc(s_yf, 1)
                wait(dve, s_yh, i, 16, 4 * q + t + 1)
                c = slice((q % 2) * P, (q % 2 + 1) * P)
                v.tensor_tensor(yl[:, q // 2, 2 * t:2 * t + 2, c], yf[:, t % 2, :, :], yh[:, q // 2, 2 * t:2 * t + 2, c],
                                ALU.subtract).then_inc(s_yl, 1)

            def gate_sum(i, q):
                wait(dve, s_gt, i, 4, q + 1)
                v.tensor_tensor(gs[:, q % 2, :], gps[:, 0:RG], gt[:, :], ALU.add).then_inc(s_gs, 1)

            STEPS = 12

            def gating(i, u, part):
                n = [0 if part == 1 else 5]

                def link(ins):
                    n[0] += 1
                    ins.then_inc(s_chain, 1)
                    wait(dve, s_chain, i, 2 * STEPS, u * STEPS + n[0])

                if part == 1:
                    wait(dve, s_gs, i, 4, 2 * u + 2)
                    link(v.scalar_tensor_tensor(out=sc[:, :, :], in0=gs[:, :, R:RG], scalar=1.0 / (SX * SW),
                                                in1=gb[:, :, :], op0=ALU.mult, op1=ALU.add))
                    pairs = sc[:, :, :].rearrange("p h (a b) -> p h a b", b=2)
                    link(v.tensor_tensor(pm[:, :, :], pairs[:, :, :, 0], pairs[:, :, :, 1], ALU.max))
                    link(v.tensor_tensor(m012[:, :, :], pm[:, :, 0:1], sc[:, :, 2:3], ALU.max))
                    link(v.tensor_tensor(m123[:, :, :], pm[:, :, 1:2], sc[:, :, 1:2], ALU.max))
                    link(v.tensor_tensor(mx[:, :, :], pm[:, :, 0:1], pm[:, :, 1:2], ALU.max))
                    v.tensor_tensor(dd[:, :, :], sc[:, :, :], mx[:, :, :].to_broadcast([P, 2, G4]),
                                    ALU.subtract).then_inc(s_dd, 1)
                    return
                wait(dve, s_ee, i, 2, u + 1)
                link(v.reduce_sum(den[:, :], ee[:, :, :], axis=AX.X))
                link(v.reciprocal(ptop[:, :], den[:, :]))
                link(v.reciprocal(itop[:, :], ptop[:, :]))
                w = cw[:, :, 0:1]
                link(v.tensor_tensor(w, ptop[:, :].rearrange("p (h a) -> p h a", a=1),
                                     itop[:, :].rearrange("p (h a) -> p h a", a=1), ALU.mult))
                v.tensor_tensor(cw[:, :, 1:2], m123[:, :, :], sc[:, :, 0:1], ALU.is_gt)
                v.tensor_tensor(cw[:, :, 2:3], pm[:, :, 1:2], pm[:, :, 0:1], ALU.is_gt)
                link(v.tensor_tensor(cw[:, :, 3:4], sc[:, :, 3:4], m012[:, :, :], ALU.is_gt))
                lo = 0
                for r, hi in enumerate(RANKS):
                    n_c = hi - lo
                    f = cw[:, :, r:r + 1].to_broadcast([P, 2, n_c])
                    e = v.scalar_tensor_tensor(out=mf[:, :, lo:hi], in0=gs[:, :, lo:hi], scalar=1.0 / SW, in1=f,
                                               op0=ALU.mult, op1=ALU.mult)
                    lo = hi
                link(e)
                v.tensor_tensor(mf[:, :, RANKS[0]:R], mf[:, :, RANKS[0]:R],
                                w.to_broadcast([P, 2, R - RANKS[0]]), ALU.mult).then_inc(s_chain, 1)
                wait(dve, s_chain, i, 2 * STEPS, (u + 1) * STEPS)
                v.tensor_copy(mhl[:, :, 0:R], mf[:, :, :]).then_inc(s_m, 1)
                wait(dve, s_m, i, 4, 2 * u + 1)
                v.tensor_tensor(mhl[:, :, R:2 * R], mf[:, :, :], mhl[:, :, 0:R], ALU.subtract).then_inc(s_m, 1)

            def b_step(i, q, first=False, last=False):
                u, j = q // 2, q % 2
                pi, pu = (i, 0) if u == 1 else (i - 1, 1)
                before = not (first and u == 0)
                y_set(i, q, 0)
                if q > 0:
                    gate_sum(i, q - 1)
                elif not first:
                    gate_sum(i - 1, 3)
                if j == 0 and before:
                    gating(pi, pu, 1)
                y_set(i, q, 1)
                if j == 0 and before:
                    gating(pi, pu, 2)
                if not (last and q == 3):
                    for b in range(2):
                        x_lo(i, q + 1, b, phase_b=True)
                y_set(i, q, 2)
                y_set(i, q, 3)
                if before:
                    residual(pi, pu, range(4 * j, 4 * j + 4), phase_b=True)

            def b_body(i, first=False, last=False):
                for q in range(4):
                    b_step(i, q, first, last)

            for b in range(2):
                x_lo(0, 0, b, phase_b=True)
            b_body(0, first=True)
            with dve.Fori(1, IB - 1) as i:
                b_body(i)
            b_body(IB - 1, last=True)
            gate_sum(IB - 1, 3)
            gating(IB - 1, 1, 1)
            gating(IB - 1, 1, 2)
            residual(IB - 1, 1, range(K), phase_b=True)

        @block.tensor
        def _(pe):
            mm = nc.tensor.matmul

            def three(dst, pairs):
                n = len(pairs)
                for k, (ah, al, bh, bl) in enumerate(pairs):
                    mm(dst, ah, bh, start=(k == 0), stop=False)
                    mm(dst, ah, bl, start=False, stop=False)
                    e = mm(dst, al, bh, start=False, stop=(k == n - 1))
                return e

            def sort_counts():
                pe.wait_ge(s_cst, 9)
                pe.wait_ge(s_sort, 3)
                mm(trps[0:NC, 0:1], own[0:NB, :], ones[0:NB, 0:1], start=True, stop=True).then_inc(s_sp, 1)

            def sort_ranks():
                pe.wait_ge(s_sort, 11)
                mm(trps[:, 0:NC], used_b[:, :], tri[:, 0:NC], start=True, stop=True)
                mm(trps[0:NC, NC:NC + 1], tri[:, 0:NC], per_c[:, 4:5], start=True, stop=True)
                mm(trps[0:NC, NC + 1:NC + 2], tri[:, NC:2 * NC], per_c[:, 3:4], start=True, stop=True
                   ).then_inc(s_sp, 1)

            def sort_rows():
                pe.wait_ge(s_sort, 15)
                for r in range(2):
                    mm(trps[0:1, r * NB:(r + 1) * NB], cols[0:NB, r:r + 1], hot[0:NB, :], start=True, stop=True)
                for r in range(3):
                    e = mm(trps[0:1, 2 * NB + r * NC:2 * NB + (r + 1) * NC], per_c[:, r:r + 1], rank_hot[:, :],
                           start=True, stop=True)
                e.then_inc(s_sp, 1)

            def z_part(i, q, ks, start_up=False):
                if ks[0] == 0:
                    wait(pe, s_xl, i, 4, q + 1)
                    wait(pe, s_zl, i, 4, q - 1)
                for k in ks:
                    if start_up:
                        pe.wait_ge(s_wl, k + 1)
                    a, b = xs[:, q % 2, k, 0:P], xs[:, q % 2, k, P:2 * P]
                    for lhs, rhs in ((a, wq_h), (a, wq_l), (b, wq_h)):
                        for h in range(2):
                            e = mm(zps[q % 2][h][:, 0:384], lhs, rhs[:, k, h * 384:(h + 1) * 384],
                                   start=(k == 0 and lhs is a and rhs is wq_h),
                                   stop=(k == K - 1 and lhs is b))
                if ks[-1] == K - 1:
                    e.then_inc(s_z, 1)

            def out_products(i, u, ms):
                wait(pe, s_ol, i, 4, 2 * u + 2)
                for m in ms:
                    wait(pe, s_ft, i, 16, 8 * u + m - 1)
                    c = slice(m * P, (m + 1) * P)
                    three(wops[m % 2][:, 0:2 * P],
                          [(wo_h[:, d, c], wo_l[:, d, c], oh[:, u, d, :], ol[:, u, d, :]) for d in range(2)]
                          ).then_inc(s_f, 1)

            def a_step(i, q, last=False):
                u, j = q // 2, q % 2
                more = not (last and q == 3)
                zz = (lambda *ks: z_part(i, q + 1, ks)) if more else (lambda *ks: None)
                r = q % 2
                before = group_before(i, u)

                def oo(n):
                    if before:
                        out_products(*before, out_share(q, n, last))

                zz(0, 1)
                wait(pe, s_zl, i, 4, q + 1)
                wait(pe, s_wcl, i, 4, q + 1)
                for c in range(4):
                    d = slice(c * P, (c + 1) * P)
                    e = three(qkps[:, d], [(zh[:, r, d], zl[:, r, d], wch[:, r, 0:P], wcl[:, r, 0:P])])
                e.then_inc(s_qk, 1)
                zz(2, 3)
                oo(0)
                wait(pe, s_qkl, i, 4, q + 1)
                wait(pe, s_ol, i, 4, q)
                three(chps[:, 0:P], [(qkh[:, c, :], qkl[:, c, :], qkh[:, 2 + c, :], qkl[:, 2 + c, :])
                                     for c in range(2)]).then_inc(s_s, 1)
                zz(4, 5)
                oo(1)
                wait(pe, s_p, i, 4, q + 1)
                nc.tensor.transpose(chps[:, 0:P], pn[:, :], ident[:, :]).then_inc(s_t, 1)
                zz(6)
                oo(2)
                wait(pe, s_ptl, i, 4, q + 1)
                three(chps[:, 0:P], [(wch[:, r, P:2 * P], wcl[:, r, P:2 * P], pth[:, :], ptl[:, :])]).then_inc(s_u, 1)
                zz(7)
                oo(3)
                wait(pe, s_ul, i, 4, q + 1)
                for c in range(2):
                    d = slice(2 * DH + c * P, 2 * DH + (c + 1) * P)
                    e = three(chps[:, c * P:(c + 1) * P], [(zh[:, r, d], zl[:, r, d], uh[:, :], ul[:, :])])
                e.then_inc(s_o, 1)

            def a_body(i, last=False):
                for q in range(4):
                    a_step(i, q, last)

            sort_counts()
            z_part(0, 0, [0], start_up=True)
            sort_ranks()
            z_part(0, 0, [1], start_up=True)
            sort_rows()
            z_part(0, 0, range(2, K), start_up=True)
            a_step(0, 0)
            a_step(0, 1)
            pe.wait_ge(s_wl, K + 2)
            pe.wait_ge(s_sort, 16)
            a_step(0, 2)
            a_step(0, 3)
            with pe.Fori(1, IA - 1) as i:
                a_body(i)
            a_body(IA - 1, last=True)
            out_products(IA - 1, 1, range(K))

            def cond_set(i, q, t, bufs):
                wait(pe, s_yf, i, 16, 4 * q + t - 3)
                x_pair = xs[:, q % 2, :, :]
                for m in range(2):
                    c = slice((2 * t + m) * P, (2 * t + m + 1) * P)
                    y_m = c2ps[t][:, m * 2 * P:(m + 1) * 2 * P]
                    n = P // len(bufs)
                    for h, b in enumerate(bufs):
                        hi = w2[:, b, 0:K * T].rearrange("p (k n) -> p k n", k=K)
                        lo = w2[:, b, K * T:].rearrange("p (k n) -> p k n", k=K)
                        at = slice(h * n, (h + 1) * n)
                        both = y_m.rearrange("p (l n) -> p l n", l=2)[:, :, at]
                        for k in range(K):
                            x_k = x_pair[:, k, :].rearrange("p (l n) -> p l n", l=2)[:, :, at]
                            mm(both, hi[:, k, c], x_k, start=(k == 0), stop=False)
                        for k in range(K):
                            e = mm(y_m[:, at], lo[:, k, c], x_pair[:, k, at], start=False, stop=(k == K - 1))
                e.then_inc(s_c2, 1)

            def gate(i, q):
                u, c = q // 2, slice((q % 2) * P, (q % 2 + 1) * P)
                wait(pe, s_yl, i, 16, 4 * q + 4)
                wait(pe, s_gs, i, 4, q)
                for k in range(K):
                    mm(gps[:, 0:2 * RG], yh[:, u, k, c], ag[:, k, :], start=(k == 0), stop=False)
                for k in range(K):
                    e = mm(gps[:, 0:RG], yl[:, u, k, c], ag[:, k, 0:RG], start=False, stop=(k == K - 1))
                e.then_inc(s_g, 1)

            def transposes(i, u):
                wait(pe, s_m, i, 4, 2 * u + 2)
                for h in range(2):
                    e = nc.tensor.transpose(mtps[:, h * P:(h + 1) * P], mhl[:, h, :], ident16[:, :])
                e.then_inc(s_mt, 1)

            def ffn_main(i, u, m):
                wait(pe, s_fs, i, 16, 8 * u + m - 1)
                c = slice(m * P, (m + 1) * P)
                for k in range(K):
                    mm(fps[m % 2][:, :], wf_h[:, k, c], yhl[:, u, k, :], start=(k == 0), stop=False)
                for k in range(K):
                    mm(fps[m % 2][:, 0:2 * P], wf_l[:, k, c], yh[:, u, k, :], start=False, stop=False)

            def ffn_lora(i, u, m):
                wait(pe, s_mT, i, 2, u + 1)
                c = slice(m * P, (m + 1) * P)
                dst = fps[m % 2][:, 0:2 * P]
                mm(dst, bl_h[:, c], mT[:, :], start=False, stop=False)
                mm(dst, bl_l[0:R, c], mT[0:R, :], start=False, stop=True).then_inc(s_f, 1)

            def ffn(i, u, ms):
                for m in ms:
                    ffn_main(i, u, m)
                    ffn_lora(i, u, m)

            def b_step(i, q, first=False):
                u, j = q // 2, q % 2
                pi, pu = (i, 0) if u == 1 else (i - 1, 1)
                before = not (first and u == 0)
                way = pe.value_load(order[0:1, bass.ds(WAY + 4 * i + q, 1)], min_val=0, max_val=3)
                rank = pe.value_load(order[0:1, bass.ds(NEED + 4 * i + q, 1)], min_val=0, max_val=NC - 1)
                pe.wait_ge(s_pw, K * rank + 2 * K)
                wait(pe, s_xl, i, 4, NP + q + 1)

                def conditioned(*bufs):
                    cond_set(i, q, 0, bufs)
                    if q > 0:
                        gate(i, q - 1)
                    elif not first:
                        gate(i - 1, 3)
                    for t in range(1, 4):
                        cond_set(i, q, t, bufs)

                with pe.If(way < 2):
                    with pe.If(way < 1):
                        conditioned(0)
                    with pe.Else():
                        conditioned(1)
                with pe.Else():
                    with pe.If(way < 3):
                        conditioned(0, 1)
                    with pe.Else():
                        conditioned(1, 0)
                if j == 0 and before:
                    transposes(pi, pu)
                if before:
                    ffn(pi, pu, range(4 * j, 4 * j + 4))

            def b_body(i, first=False):
                for q in range(4):
                    b_step(i, q, first)

            pe.wait_ge(s_order, 1)
            pe.wait_ge(s_wl, NCH)
            pe.wait_ge(s_res, FA)
            pe.wait_ge(s_pw, K)
            pe.sem_inc(s_c2, 1)
            b_body(0, first=True)
            with pe.Fori(1, IB - 1) as i:
                b_body(i)
            b_body(IB - 1)
            gate(IB - 1, 3)
            for m in range(2):
                ffn_main(IB - 1, 1, m)
            transposes(IB - 1, 1)
            for m in range(2):
                ffn_lora(IB - 1, 1, m)
            ffn(IB - 1, 1, range(2, K))


def kernel(x, itok_B_0_15, L0_cond_weights, L0_attn_Wqkv, L0_attn_bqkv, L0_attn_Wo, L0_attn_bo, L0_cond2_weight,
           L0_ffn_W, L0_ffn_b, L0_ffn_A, L0_ffn_B, L0_ffn_gate_w, L0_ffn_gate_b):
    import numpy as np
    from concourse import bacc
    from concourse.bass_utils import run_bass_kernel_spmd

    a = {n: np.asarray(v) for n, v in locals().items() if n not in ("np", "bacc", "run_bass_kernel_spmd")}
    x = a["x"]
    NB = x.shape[0]

    def chunked(w):
        return np.ascontiguousarray(w.reshape(-1, P, w.shape[1]).transpose(1, 0, 2).reshape(P, -1))

    wc = a["L0_cond_weights"]
    bias = np.concatenate([a[n].reshape(-1, P).T for n in ("L0_attn_bqkv", "L0_attn_bo", "L0_ffn_b")], axis=1)
    bt = a["L0_ffn_B"].T
    arrays = {
        "x_in": x.reshape(NB // 4, 4, S, K, P).transpose(0, 4, 1, 3, 2).reshape(NB // 4, P, GR),
        "ids_in": a["itok_B_0_15"].reshape(1, NB),
        "wc_in": np.stack([wc, wc.transpose(0, 2, 1)], axis=2),
        "wqkv_in": chunked(a["L0_attn_Wqkv"]),
        "wo_in": chunked(a["L0_attn_Wo"]),
        "w2_in": a["L0_cond2_weight"].transpose(0, 2, 1).reshape(NC, K, P, T).transpose(0, 2, 1, 3).reshape(NC, P, K * T),
        "w_in": chunked(a["L0_ffn_W"].T),
        "ag_in": chunked(np.concatenate([a["L0_ffn_A"], a["L0_ffn_gate_w"]], axis=0).T),
        "bl_in": np.concatenate([bt, bt], axis=0),
        "bias_in": bias,
        "gb_in": a["L0_ffn_gate_b"].reshape(1, G4),
    }
    arrays = {n: np.ascontiguousarray(v) for n, v in arrays.items()}
    nc = bacc.Bacc("TRN2", target_bir_lowering=False, num_devices=1)
    args = {n: nc.dram_tensor(n, v.shape, mybir.dt.from_np(v.dtype), kind="ExternalInput").ap()
            for n, v in arrays.items()}
    out = nc.dram_tensor("out", [NB, P, BT], F32, kind="ExternalOutput").ap()
    x1 = nc.dram_tensor("x1", [NB, P, BT], F32, kind="Internal").ap()
    build(nc, NB, out=out, x1=x1, **args)
    r = run_bass_kernel_spmd(nc, [arrays], core_ids=[0])
    got = np.asarray(r.results[0]["out"])
    return np.ascontiguousarray(got.reshape(NB, P, K, S).transpose(0, 3, 2, 1)).reshape(NB, S, T)
```
